# Optimizing a Trainium2 kernel written in Bass

```python
import numpy as np
import jax
import jax.numpy as jnp

def _softmax(x, axis=-1):
    return jax.nn.softmax(x, axis=axis)

def _gelu(x):
    return jax.nn.gelu(x, approximate=True)

def _silu(x):
    return jax.nn.silu(x)

def _sigmoid(x):
    return jax.nn.sigmoid(x)

def _layernorm(x, axis=-1, eps=1e-05):
    m = jnp.mean(x, axis=axis, keepdims=True)
    v = jnp.var(x, axis=axis, keepdims=True)
    return (x - m) / jnp.sqrt(v + eps)

def _scatter_add(tgt, idx, src, axis=0):
    return tgt.at[idx].add(src)

def _segment_sum(src, seg, n):
    return jax.ops.segment_sum(src, seg, n)
kernel_name = 'mk_flamingo_gated_d1_seqx_r4_b0e26b'

def setup_inputs(seed: int=0):
    np.random.seed(seed)
    _w = jnp.asarray

    def _rec_inputs():
        import jax
        import jax.numpy as jnp
        _rk = jax.random.key(seed)
        x = -0.0003929 + 0.9999 * jax.random.normal(jax.random.fold_in(_rk, 1), (16, 128, 1024), jnp.float32)
        _lenS = 128 - jax.random.randint(jax.random.fold_in(_rk, 7), (16,), 0, max(1, 128 // 4) + 1, jnp.int32)
        _lenS2 = 128 - jax.random.randint(jax.random.fold_in(_rk, 8), (16,), 0, max(1, 128 // 4) + 1, jnp.int32)
        _ctx_4096P = jax.random.normal(jax.random.fold_in(_rk, 11), (16, 16, 1024), jnp.float32)
        _ctx_4096c = jax.random.dirichlet(jax.random.fold_in(_rk, 511), 0.3 * jnp.ones((16,), jnp.float32), (16, 128))
        _ctx_4096t = jnp.einsum('bsk,bkd->bsd', _ctx_4096c, _ctx_4096P)
        _ctx_4096t = _ctx_4096t * jax.lax.rsqrt(jnp.mean(jnp.square(_ctx_4096t)) + 1e-12) * 0.953939
        ctx_4096 = 2.81802e-05 + 1.00001 * (_ctx_4096t + 0.3 * jax.random.normal(jax.random.fold_in(_rk, 611), (16, 128, 1024), jnp.float32))
        _g = jax.random.normal(jax.random.fold_in(_rk, 9001), (2, 1), jnp.float32)
        _g = jnp.sign(_g) * jnp.maximum(jnp.abs(_g), 1.0) + (_g == 0) * 1.0
        g_xattn = _g[0]
        g_ffn = _g[1]
        return (x, ctx_4096, g_xattn, g_ffn)
    x, ctx_4096, g_xattn, g_ffn = _rec_inputs()

    def _L0_xattn_setup():
        import jax, jax.numpy as jnp
        import numpy as np
        EPS = 1e-08

        def _cosine_sim(a, b):
            na = jnp.maximum(jnp.sqrt(jnp.sum(a * a, axis=1)), EPS)
            nb = jnp.maximum(jnp.sqrt(jnp.sum(b * b, axis=1)), EPS)
            return jnp.sum(a * b, axis=1) / (na * nb)
        key = jax.random.key(seed)
        k1, k2, k3 = jax.random.split(key, 3)
        B, C, T, O, K = (8, 128, 1024, 128, 3)
        feature = jax.random.normal(k1, (B, C, T), dtype=jnp.float32)
        embedding = jax.random.normal(k2, (B, C, T), dtype=jnp.float32)
        weight = jax.random.normal(k3, (O, C, K), dtype=jnp.float32) * 0.05
        return {'feature': feature, 'embedding': embedding, 'weight': weight}
    _L0_xattn_all = _L0_xattn_setup()
    _L0_xattn_in = {k: v for k, v in _L0_xattn_all.items() if k in ('weight',)}
    del _L0_xattn_all

    def _L0_ffn_setup():
        import jax, jax.numpy as jnp
        import numpy as np
        B_, S, D = (4, 1024, 1024)
        E, R, O = (8, 16, 1024)
        TOP_K = 2
        SCALING = 8.0 / R
        key = jax.random.key(seed)
        ks = jax.random.split(key, 5)
        x = jax.random.normal(ks[0], (B_, S, D), dtype=jnp.float32)
        router_w = jax.random.normal(ks[1], (E, D), dtype=jnp.float32) * (1.0 / np.sqrt(D))
        router_b = jax.random.normal(ks[2], (E,), dtype=jnp.float32) * 0.01
        A = jax.random.normal(ks[3], (E, R, D), dtype=jnp.float32) * (1.0 / np.sqrt(D))
        Bm = jax.random.normal(ks[4], (E, O, R), dtype=jnp.float32) * 0.02
        return {'x': x, 'router_w': router_w, 'router_b': router_b, 'A': A, 'Bm': Bm}
    _L0_ffn_all = _L0_ffn_setup()
    _L0_ffn_in = {k: v for k, v in _L0_ffn_all.items() if k in ('router_w', 'router_b', 'A', 'Bm')}
    del _L0_ffn_all
    return {'x': x, 'ctx_4096': ctx_4096, 'g_xattn': g_xattn, 'g_ffn': g_ffn, 'L0_xattn_weight': _L0_xattn_in['weight'], 'L0_ffn_router_w': _L0_ffn_in['router_w'], 'L0_ffn_router_b': _L0_ffn_in['router_b'], 'L0_ffn_A': _L0_ffn_in['A'], 'L0_ffn_Bm': _L0_ffn_in['Bm']}

def reference(x, ctx_4096, g_xattn, g_ffn, L0_xattn_weight, L0_ffn_router_w, L0_ffn_router_b, L0_ffn_A, L0_ffn_Bm):
    import jax
    import jax.numpy as jnp

    def _L0_xattn_ref(feature, embedding, weight):
        import jax, jax.numpy as jnp
        import numpy as np
        EPS = 1e-08

        def _cosine_sim(a, b):
            na = jnp.maximum(jnp.sqrt(jnp.sum(a * a, axis=1)), EPS)
            nb = jnp.maximum(jnp.sqrt(jnp.sum(b * b, axis=1)), EPS)
            return jnp.sum(a * b, axis=1) / (na * nb)
        B, C, T = feature.shape
        O = weight.shape[0]
        K = 3
        emb_l = jnp.pad(embedding[:, :, :-1], ((0, 0), (0, 0), (1, 0)))
        emb_r = jnp.pad(embedding[:, :, 1:], ((0, 0), (0, 0), (0, 1)))
        sim = jnp.stack([_cosine_sim(embedding, emb_l), _cosine_sim(embedding, embedding), _cosine_sim(embedding, emb_r)], axis=1)
        att = jnp.repeat(sim, C, axis=1)
        f_pad = jnp.pad(feature, ((0, 0), (0, 0), (1, 1)))
        inp_unf = jnp.stack([f_pad[:, :, k:k + T] for k in range(K)], axis=2)
        inp_unf = inp_unf.reshape(B, C * K, T)
        w_flat = weight.reshape(O, C * K)
        out = jnp.einsum('bit,oi->bot', inp_unf * att, w_flat)
        return out

    def _L0_ffn_ref(x, router_w, router_b, A, Bm):
        import jax, jax.numpy as jnp
        import numpy as np
        B_, S, D = (4, 1024, 1024)
        E, R, O = (8, 16, 1024)
        TOP_K = 2
        SCALING = 8.0 / R
        flat = x.reshape(-1, x.shape[-1])
        N = flat.shape[0]
        logits = flat @ router_w.T + router_b
        probs = jax.nn.softmax(logits, axis=-1)
        topv, topi = jax.lax.top_k(probs, TOP_K)
        gates = topv / jnp.sum(topv, axis=-1, keepdims=True)
        w = jnp.zeros((N, E), dtype=flat.dtype).at[jnp.arange(N)[:, None], topi].add(gates)
        h = jnp.einsum('nd,erd->ner', flat, A)
        hw = h * w[:, :, None]
        out = jnp.einsum('ner,eor->no', hw, Bm) * SCALING
        return out.reshape(*x.shape[:-1], O)
    x = x + jnp.tanh(g_xattn[0]) * _L0_xattn_ref(_layernorm(x, axis=-1), ctx_4096, L0_xattn_weight)
    x = x + jnp.tanh(g_ffn[0]) * _L0_ffn_ref(_layernorm(x, axis=-1), L0_ffn_router_w, L0_ffn_router_b, L0_ffn_A, L0_ffn_Bm)
    return x

_drawn_inputs = setup_inputs


def setup_inputs(seed=0):
    import zlib

    import numpy as np

    out = dict(_drawn_inputs(seed))
    spreads = {}
    factors = {}
    for name, (base, spread) in spreads.items():
        noise = np.random.default_rng([zlib.crc32(name.encode()), seed]).standard_normal(out[name].shape)
        drawn = base * np.exp(spread * noise) if base else spread * noise
        out[name] = jnp.asarray(drawn.astype(out[name].dtype))
    for name, factor in factors.items():
        out[name] = (out[name] * factor).astype(out[name].dtype)
    return out
```

```python
import concourse.bass as bass
from concourse import mybir
from contextlib import ExitStack

F32 = mybir.dt.float32
BF16 = mybir.dt.bfloat16
U32 = mybir.dt.uint32
ALU = mybir.AluOpType
ACT = mybir.ActivationFunctionType

P = 128
HALF = 512
LN_EPS = 1e-5
COS_EPS = 1e-8
TAPS = 3
G = 4
TAP_ORDER = (1, 0, 2)


def flamingo_kernel(nc, x, ctx, g_xattn, g_ffn, conv_wT, expert_aT, router_b, expert_b,
                    identity, identity_bf, one_hot, shift, select, expert_ids, out):
    B, C, T = x.shape
    NG = B // G
    KC = T // P
    E = router_b.shape[0]
    ER = expert_aT.shape[2] - E
    R = ER // E
    SCALING = 8.0 / R
    assert C == P and T == 2 * HALF and ER == P and B % G == 0 and NG >= 3

    st = ExitStack()
    with st:
        def sb(name, shape, dt=F32):
            return st.enter_context(nc.sbuf_tensor(name, shape, dt))

        def sem(name):
            return st.enter_context(nc.semaphore(name))

        ident = sb("ident", [P, P])
        identb = sb("identb", [P, P], BF16)
        onehot = sb("onehot", [P, G, 32])
        shifts = sb("shifts", [P, 2, P])
        sel = sb("sel", [96, G, TAPS, P], BF16)
        ids = sb("ids", [P, E])
        mean_w = sb("mean_w", [P, P])
        minus_half = sb("minus_half", [P, KC * G])
        eps = sb("eps", [P, 1])
        gates_in = sb("gates_in", [P, 2])
        gates_th = sb("gates_th", [P, 2])
        wT_in = sb("wT_in", [P, TAPS * P])
        wT = sb("wT", [P, TAPS * P])
        aT_in = sb("aT_in", [P, KC, ER + E])
        aT = sb("aT", [P, KC, ER + E])
        rb = sb("rb", [P, E])
        bm_in = sb("bm_in", [P, T])
        bm = sb("bm", [P, T])
        et = sb("et", [P, G, T])
        sq = sb("sq", [P, 2, T])
        pr = sb("pr", [P, 2, T])
        sums = sb("sums", [P, HALF])
        nd = sb("nd", [P, 4, G, G])
        nmax = sb("nmax", [P, KC, G])
        rinv = sb("rinv", [P, KC, G])
        dr = sb("dr", [P, KC, G])
        nr = sb("nr", [P, KC, G])
        sim = sb("sim", [P, KC, 3, G])
        rest1 = sb("rest1", [P, KC, 3, G])
        rest2 = sb("rest2", [P, KC, 3, G])
        simp = sb("simp", [P, KC, 3, 32], BF16)
        rows = sb("rows", [96, NG, T], BF16)
        xt = sb("xt", [P, G, T])
        x1 = sb("x1", [P, G, T])
        bn1 = sb("bn1", [P, 2, 12])
        mv1 = sb("mv1", [P, G, 2])
        ve1 = sb("ve1", [P, G])
        rs1 = sb("rs1", [P, G])
        wb = sb("wb", [P, 2, TAPS, P])
        pt = sb("pt", [P, 4, HALF])
        bn2 = sb("bn2", [P, 2, 12])
        mv2 = sb("mv2", [P, 2, 2])
        ve2 = sb("ve2", [P, 2])
        rs2 = sb("rs2", [P, 2])
        xT = sb("xT", [P, 2, KC, P])
        logit = sb("logit", [P, E])
        top = sb("top", [P, 8])
        topi = sb("topi", [P, 8], U32)
        below = sb("below", [P, E])
        expo = sb("expo", [P, E])
        pick0 = sb("pick0", [P, E])
        pick = sb("pick", [P, E])
        expk = sb("expk", [P, E])
        esum = sb("esum", [P, 1])
        einv = sb("einv", [P, 1])
        gate = sb("gate", [P, E])
        hw = sb("hw", [P, 2, ER])
        hwT = sb("hwT", [P, 2, P])

        bank = [st.enter_context(nc.psum_tensor(f"bank{i}", [P, HALF], F32)) for i in range(8)]
        sim_ps = bank[0:2]
        conv_ps = bank[2:4]
        xT_ps = bank[4]
        out_ps = bank[5]
        h_ps = bank[6][:, 0:ER + E]
        hwT_ps = bank[6][:, 256:256 + P]
        sum_ps = bank[7]
        ctxT_ps = bank[7][:, :].rearrange("p (w q b) -> p q w b", w=4, q=4)
        rnext_ps = bank[7][:, 0:KC * G]
        rows_ps = bank[7][:, :].bitcast(BF16)

        const_in = sem("const_in")
        onehot_in = sem("onehot_in")
        e_in = [sem(f"e_in{j}") for j in range(G)]
        x_in = [sem(f"x_in{j}") for j in range(G)]
        stored = [sem(f"stored{j}") for j in range(G)]
        setup = sem("setup")
        tanh_done = sem("tanh_done")
        mean_done = sem("mean_done")
        weights_done = sem("weights_done")
        sq_done = sem("sq_done")
        pr_done = sem("pr_done")
        summed = sem("summed")
        sums_out = sem("sums_out")
        ctxT_done = sem("ctxT_done")
        nd_done = sem("nd_done")
        nmax_done = sem("nmax_done")
        rinv_done = sem("rinv_done")
        rnext_done = sem("rnext_done")
        partial = sem("partial")
        sim_done = sem("sim_done")
        split = sem("split")
        rowsT_done = sem("rowsT_done")
        rows_done = sem("rows_done")
        bn1_done = sem("bn1_done")
        mv1_done = sem("mv1_done")
        ve1_done = sem("ve1_done")
        rs1_done = sem("rs1_done")
        wb_done = sem("wb_done")
        spread = sem("spread")
        mod_done = sem("mod_done")
        tap_done = sem("tap_done")
        x1_done = sem("x1_done")
        bn2_done = sem("bn2_done")
        mv2_done = sem("mv2_done")
        ve2_done = sem("ve2_done")
        rs2_done = sem("rs2_done")
        xT_done = sem("xT_done")
        xT_out = sem("xT_out")
        h_done = sem("h_done")
        logit_done = sem("logit_done")
        top_done = sem("top_done")
        topi_done = sem("topi_done")
        below_done = sem("below_done")
        expo_done = sem("expo_done")
        pick0_done = sem("pick0_done")
        pick_done = sem("pick_done")
        esum_done = sem("esum_done")
        einv_done = sem("einv_done")
        gate_done = sem("gate_done")
        hw_done = sem("hw_done")
        hwT_done = sem("hwT_done")
        hwT_out = sem("hwT_out")
        ffn_done = sem("ffn_done")
        out_done = sem("out_done")
        N_CONST = 11

        block = st.enter_context(nc.Block())

        def each_group(eng, body):
            body(0, True, False)
            with eng.Fori(1, NG - 1) as g:
                body(g, False, False)
            body(NG - 1, False, True)

        def past(g, j, k):
            return not isinstance(g, int) or G * g + j >= k

        def half(h):
            return slice(h * HALF, (h + 1) * HALF)

        @block.sync
        def _(sp):
            def load_e(g, j):
                if past(g, 0, 1):
                    sp.wait_ge(sq_done, G * g + j - G + 1)
                    sp.wait_ge(pr_done, G * g + j - G + 1)
                sp.dma_start(et[:, j, :], ctx[G * g + j, :, :]).then_inc(e_in[j], 16)

            def load_x(g, j):
                if past(g, 0, 1):
                    sp.wait_ge(x1_done, 2 * (G * g + j - G + 1))
                sp.dma_start(xt[:, j, :], x[G * g + j, :, :]).then_inc(x_in[j], 16)

            def store(g, j):
                sp.wait_ge(out_done, 2 * (G * g + j + 1))
                sp.dma_start(out[G * g + j, :, :], x1[:, j, :]).then_inc(stored[j], 16)

            load_e(0, 0)
            load_e(0, 1)
            sp.dma_start(onehot[:, :, :], one_hot).then_inc(onehot_in, 16)
            load_e(0, 2)
            load_e(0, 3)
            sp.dma_start(ident[:, :], identity).then_inc(const_in, 16)
            load_x(0, 0)
            sp.dma_start(identb[:, :], identity_bf).then_inc(const_in, 16)
            sp.dma_start(shifts[:, :, :], shift).then_inc(const_in, 16)
            sp.dma_start(sel[:, :, :, :], select).then_inc(const_in, 16)
            sp.dma_start(wT_in[:, :], conv_wT).then_inc(const_in, 16)
            sp.dma_start(gates_in[:, 0:1], g_xattn.rearrange("(a n) -> a n", a=1).to_broadcast([P, 1])).then_inc(const_in, 16)
            sp.dma_start(gates_in[:, 1:2], g_ffn.rearrange("(a n) -> a n", a=1).to_broadcast([P, 1])).then_inc(const_in, 16)
            sp.dma_start(ids[:, :], expert_ids).then_inc(const_in, 16)
            sp.dma_start(rb[:, :], router_b.rearrange("(a n) -> a n", a=1).to_broadcast([P, E])).then_inc(const_in, 16)
            sp.dma_start(aT_in[:, :, :], expert_aT).then_inc(const_in, 16)
            load_x(0, 1)
            load_x(0, 2)
            sp.dma_start(bm_in[:, :], expert_b).then_inc(const_in, 16)
            for j in range(G):
                load_e(1, j)
            load_x(0, 3)

            def body(g, first, last):
                for j in range(G):
                    if j > 0 and not last:
                        load_x(g + 1, j - 1)
                    if j == 0 and not first:
                        load_x(g, G - 1)
                    if j == 1 and not last and not (isinstance(g, int) and g + 2 >= NG):
                        load_e(g + 2, 0)
                        load_e(g + 2, 1)
                    if j == 2 and not last and not (isinstance(g, int) and g + 2 >= NG):
                        load_e(g + 2, 2)
                        load_e(g + 2, 3)
                    if j >= 2:
                        store(g, j - 2)
                    elif not first:
                        store(g - 1, j + 2)

            body(0, True, False)
            with sp.Fori(1, NG - 2) as g:
                body(g, False, False)
            body(NG - 2, False, False)
            body(NG - 1, False, True)
            store(NG - 1, G - 2)
            store(NG - 1, G - 1)
            for j in range(G):
                sp.wait_ge(stored[j], 16 * NG)

        @block.gpsimd
        def _(pool):
            nc.gpsimd.memset(eps[:, :], LN_EPS).then_inc(setup, 1)
            nc.gpsimd.memset(minus_half[:, :], -0.5).then_inc(setup, 1)
            nc.gpsimd.memset(mean_w[:, :], 1.0 / T).then_inc(setup, 1)
            nc.gpsimd.memset(pr[:, :, T - 1:T], 0.0).then_inc(setup, 1)
            nc.gpsimd.memset(simp[:, :, :, :], 0.0).then_inc(setup, 1)
            nc.gpsimd.memset(rows[:, :, :], 0.0).then_inc(setup, 1)
            pool.wait_ge(setup, 6)

            def product(g, j):
                if past(g, j, 2):
                    pool.wait_ge(summed, G * g + j - 1)
                pool.wait_ge(e_in[j], 16 * (g + 1))
                nc.gpsimd.tensor_tensor(pr[:, j % 2, 0:T - 1], et[:, j, 0:T - 1], et[:, j, 1:T],
                                        ALU.mult).then_inc(pr_done, 1)

            def inverse_norms(g):
                pool.wait_ge(nmax_done, g + 1)
                nc.gpsimd.tensor_tensor(rinv[:, :, :].rearrange("p a b -> p (a b)"),
                                        nmax[:, :, :].rearrange("p a b -> p (a b)"),
                                        minus_half[:, :], ALU.pow).then_inc(rinv_done, 1)

            def feature_rstd(g, j):
                pool.wait_ge(mv1_done, G * g + j + 1)
                nc.gpsimd.tensor_tensor(ve1[:, j:j + 1], mv1[:, j, 1:2], eps[:, :], ALU.add).then_inc(ve1_done, 1)
                pool.wait_ge(ve1_done, G * g + j + 1)
                nc.gpsimd.tensor_tensor(rs1[:, j:j + 1], ve1[:, j:j + 1], minus_half[:, 0:1],
                                        ALU.pow).then_inc(rs1_done, 1)

            def token_rstd(g, j):
                i = j % 2
                pool.wait_ge(mv2_done, G * g + j + 1)
                nc.gpsimd.tensor_tensor(ve2[:, i:i + 1], mv2[:, i, 1:2], eps[:, :], ALU.add).then_inc(ve2_done, 1)
                pool.wait_ge(ve2_done, G * g + j + 1)
                nc.gpsimd.tensor_tensor(rs2[:, i:i + 1], ve2[:, i:i + 1], minus_half[:, 0:1],
                                        ALU.pow).then_inc(rs2_done, 1)

            for j in range(G):
                product(0, j)
            inverse_norms(0)
            feature_rstd(0, 0)
            feature_rstd(0, 1)

            def body(g, first, last):
                for j in range(G):
                    if j < 2 and not last:
                        product(g + 1, 2 * j)
                    if j > 0:
                        token_rstd(g, j - 1)
                    elif not first:
                        token_rstd(g - 1, G - 1)
                    if j < 2:
                        feature_rstd(g, j + 2)
                        if not last:
                            product(g + 1, 2 * j + 1)
                    elif not last:
                        if j == 2:
                            inverse_norms(g + 1)
                        feature_rstd(g + 1, j - 2)

            each_group(pool, body)
            token_rstd(NG - 1, G - 1)

        @block.scalar
        def _(act):
            def square(g, j):
                if past(g, j, 2):
                    act.wait_ge(summed, G * g + j - 1)
                act.wait_ge(e_in[j], 16 * (g + 1))
                nc.scalar.activation(sq[:, j % 2, :], et[:, j, :], ACT.Square).then_inc(sq_done, 1)

            def sums_evacuate(g):
                act.wait_ge(summed, G * (g + 1))
                if past(g, 0, 1):
                    act.wait_ge(ctxT_done, g)
                nc.scalar.activation(sums[:, :], sum_ps[:, :], ACT.Copy).then_inc(sums_out, 1)

            def rows_evacuate(g):
                act.wait_ge(rowsT_done, g + 1)
                nc.scalar.activation(rows[64:96, g, 1:T], rows_ps[64:96, 0:T - 1], ACT.Copy).then_inc(rows_done, 1)
                nc.scalar.activation(rows[0:64, g, :], rows_ps[0:64, :], ACT.Copy).then_inc(rows_done, 1)

            def scale_weights(g, j):
                act.wait_ge(rs1_done, G * g + j + 1)
                if past(g, j, 2):
                    act.wait_ge(tap_done, 6 * (G * g + j - 1))
                nc.scalar.activation(wb[:, j % 2, :, :].rearrange("p k o -> p (k o)"), wT[:, :], ACT.Copy,
                                     scale=rs1[:, j:j + 1]).then_inc(wb_done, 1)

            def tokens_evacuate(g, j, h):
                act.wait_ge(xT_done, 2 * (G * g + j) + h + 1)
                if past(g, j, 2):
                    act.wait_ge(h_done, G * g + j - 1)
                nc.scalar.activation(xT[:, j % 2, 4 * h:4 * h + 4, :].rearrange("p c n -> p (c n)"),
                                     xT_ps[:, :], ACT.Copy).then_inc(xT_out, 1)

            def exponent(g, j):
                act.wait_ge(below_done, G * g + j + 1)
                if past(g, j, 1):
                    act.wait_ge(esum_done, G * g + j)
                nc.scalar.activation(expo[:, :], below[:, :], ACT.Exp).then_inc(expo_done, 1)

            def hidden_evacuate(g, j):
                act.wait_ge(hwT_done, G * g + j + 1)
                if past(g, j, 2):
                    act.wait_ge(ffn_done, 2 * (G * g + j - 1))
                nc.scalar.activation(hwT[:, j % 2, :], hwT_ps, ACT.Copy).then_inc(hwT_out, 1)

            square(0, 0)
            square(0, 1)
            square(0, 2)
            square(0, 3)
            act.wait_ge(const_in, 16 * N_CONST)
            nc.scalar.activation(gates_th[:, :], gates_in[:, :], ACT.Tanh).then_inc(tanh_done, 1)
            sums_evacuate(0)
            act.wait_ge(weights_done, 1)
            scale_weights(0, 0)
            act.wait_ge(setup, 6)
            rows_evacuate(0)

            def body(g, first, last):
                for j in range(G):
                    def before(k):
                        return (g, j - k) if j >= k else (g - 1, j - k + G)
                    if j < 2 and not last:
                        square(g + 1, 2 * j)
                    if j >= 2 or not first:
                        hidden_evacuate(*before(2))
                    if j >= 1 or not first:
                        tokens_evacuate(*before(1), 0)
                        tokens_evacuate(*before(1), 1)
                    if j < 3 :
                        scale_weights(g, j + 1)
                    elif not last:
                        scale_weights(g + 1, 0)
                    if j < 2 and not last:
                        square(g + 1, 2 * j + 1)
                    if j == 2 and not last:
                        sums_evacuate(g + 1)
                    if j == 3 and not last:
                        rows_evacuate(g + 1)
                    if j >= 1 or not first:
                        exponent(*before(1))

            each_group(act, body)
            hidden_evacuate(NG - 1, G - 2)
            tokens_evacuate(NG - 1, G - 1, 0)
            tokens_evacuate(NG - 1, G - 1, 1)
            exponent(NG - 1, G - 1)
            hidden_evacuate(NG - 1, G - 1)

        @block.vector
        def _(dve):
            def feature_stats(g, j, h):
                if h == 0:
                    dve.wait_ge(x_in[j], 16 * (g + 1))
                nc.vector.bn_stats(bn1[:, j % 2, 6 * h:6 * h + 6], xt[:, j, half(h)]).then_inc(bn1_done, 1)

            def feature_stats_in(g, j):
                dve.wait_ge(bn1_done, 2 * (G * g + j + 1))
                if past(g, 0, 1):
                    dve.wait_ge(rs1_done, G * g + j - G + 1)

            def feature_mean(g, j):
                nc.vector.bn_aggr(mv1[:, j, :], bn1[:, j % 2, :]).then_inc(mv1_done, 1)

            def context_columns(g):
                dve.wait_ge(ctxT_done, g + 1)
                nc.vector.tensor_copy(nd[:, :, :, :], ctxT_ps[:, :, :, 0:G]).then_inc(nd_done, 1)
                dve.wait_ge(nd_done, g + 1)
                nc.vector.tensor_scalar(nmax[:, :, :].rearrange("p a b -> p (a b)"),
                                        nd[:, 0:2, :, :].rearrange("p h w b -> p (h w b)"),
                                        COS_EPS * COS_EPS, None, ALU.max).then_inc(nmax_done, 1)

            norms = nd[:, 0:2, :, :].rearrange("p h w b -> p (h w) b")
            dots = nd[:, 2:4, :, :].rearrange("p h w b -> p (h w) b")

            def similarities(g):
                dve.wait_ge(rinv_done, g + 1)
                nc.vector.tensor_tensor(dr[:, :, :], dots, rinv[:, :, :], ALU.mult).then_inc(partial, 1)
                nc.vector.tensor_tensor(nr[:, :, :], norms, rinv[:, :, :], ALU.mult).then_inc(partial, 1)
                dve.wait_ge(rnext_done, g + 1)
                dve.wait_ge(partial, 2 * (g + 1))
                nc.vector.tensor_tensor(sim[:, :, 0:3:2, :],
                                        dr[:, :, :].unsqueeze(2).to_broadcast([P, KC, 2, G]),
                                        rnext_ps.rearrange("p (a b) -> p a b", b=G).unsqueeze(2).to_broadcast([P, KC, 2, G]),
                                        ALU.mult).then_inc(sim_done, 1)
                nc.vector.tensor_tensor(sim[:, :, 1, :], nr[:, :, :], rinv[:, :, :], ALU.mult).then_inc(sim_done, 1)

            def split_similarities(g):
                part = [simp[:, :, :, G * i:G * i + G] for i in range(3)]
                dve.wait_ge(sim_done, 2 * (g + 1))
                nc.vector.tensor_copy(part[0], sim[:, :, :, :]).then_inc(split, 1)
                yield
                dve.wait_ge(split, 5 * g + 1)
                nc.vector.tensor_tensor(rest1[:, :, :, :], sim[:, :, :, :], part[0], ALU.subtract).then_inc(split, 1)
                yield
                dve.wait_ge(split, 5 * g + 2)
                nc.vector.tensor_copy(part[1], rest1[:, :, :, :]).then_inc(split, 1)
                yield
                dve.wait_ge(split, 5 * g + 3)
                nc.vector.tensor_tensor(rest2[:, :, :, :], rest1[:, :, :, :], part[1], ALU.subtract).then_inc(split, 1)
                yield
                dve.wait_ge(split, 5 * g + 4)
                nc.vector.tensor_copy(part[2], rest2[:, :, :, :]).then_inc(split, 1)
                yield

            def modulate(g, j, i):
                n = 6 * (G * g + j) + i
                h, k = i // 3, TAP_ORDER[i % 3]
                lo = 1 if (k == 0 and h == 0) else 0
                hi = HALF - 1 if (k == 2 and h == 1) else HALF
                c = h * HALF + k - 1
                dve.wait_ge(spread, n + 1)
                if not (isinstance(g, int) and n < 4):
                    dve.wait_ge(tap_done, n - 3)
                nc.vector.scalar_tensor_tensor(
                    out=pt[:, (6 * j + i) % 4, lo:hi],
                    in0=xt[:, j, c + lo:c + hi], scalar=mv1[:, j, 0:1], in1=sim_ps[i % 2][:, lo:hi],
                    op0=ALU.subtract, op1=ALU.mult).then_inc(mod_done, 1)

            def residual(g, j, h):
                n = G * g + j
                dve.wait_ge(tap_done, 6 * n + 3 * (h + 1))
                if h == 0 and not (isinstance(g, int) and g == 0):
                    dve.wait_ge(stored[j], 16 * g)
                nc.vector.tensor_tensor(x1[:, j, half(h)], conv_ps[h][:, :], xt[:, j, half(h)],
                                        ALU.add).then_inc(x1_done, 1)

            def token_stats(g, j, h):
                n = G * g + j
                dve.wait_ge(x1_done, 2 * n + h + 1)
                nc.vector.bn_stats(bn2[:, j % 2, 6 * h:6 * h + 6], x1[:, j, half(h)]).then_inc(bn2_done, 1)

            def token_stats_in(g, j):
                dve.wait_ge(bn2_done, 2 * (G * g + j + 1))

            def logits_in(g, j):
                dve.wait_ge(logit_done, G * g + j + 1)

            def token_variance(g, j):
                nc.vector.bn_aggr(mv2[:, j % 2, :], bn2[:, j % 2, :]).then_inc(mv2_done, 1)

            def gating(g, j):
                n = G * g + j
                rstd = rs2[:, j % 2:j % 2 + 1]
                dve.wait_ge(rs2_done, n + 1)
                dve.wait_ge(h_done, n + 1)
                nc.vector.scalar_tensor_tensor(out=logit[:, :], in0=h_ps[:, ER:ER + E], scalar=rstd, in1=rb[:, :],
                                               op0=ALU.mult, op1=ALU.add).then_inc(logit_done, 1)
                yield
                nc.vector.max(top[:, :], logit[:, :]).then_inc(top_done, 1)
                yield
                dve.wait_ge(top_done, n + 1)
                nc.vector.tensor_scalar(below[:, :], logit[:, :], top[:, 0:1], None, ALU.subtract).then_inc(below_done, 1)
                nc.vector.max_index(topi[:, :], top[:, :], logit[:, :]).then_inc(topi_done, 1)
                yield
                dve.wait_ge(topi_done, n + 1)
                nc.vector.tensor_scalar(pick0[:, :], ids[:, :], topi[:, 0:1], None, ALU.is_equal).then_inc(pick0_done, 1)
                yield
                dve.wait_ge(pick0_done, n + 1)
                nc.vector.scalar_tensor_tensor(out=pick[:, :], in0=ids[:, :], scalar=topi[:, 1:2], in1=pick0[:, :],
                                               op0=ALU.is_equal, op1=ALU.add).then_inc(pick_done, 1)
                yield
                dve.wait_ge(pick_done, n + 1)
                dve.wait_ge(expo_done, n + 1)
                nc.vector.scalar_tensor_tensor(out=expk[:, :], in0=expo[:, :], scalar=1.0, in1=pick[:, :],
                                               op0=ALU.mult, op1=ALU.mult, accum_out=esum[:, :]).then_inc(esum_done, 1)
                yield
                dve.wait_ge(esum_done, n + 1)
                nc.vector.reciprocal(einv[:, :], esum[:, :]).then_inc(einv_done, 1)
                yield
                dve.wait_ge(einv_done, n + 1)
                nc.vector.tensor_scalar(gate[:, :], expk[:, :], einv[:, :], rstd, ALU.mult, ALU.mult).then_inc(gate_done, 1)
                yield
                dve.wait_ge(gate_done, n + 1)
                if past(g, j, 2):
                    dve.wait_ge(hwT_done, n - 1)
                nc.vector.tensor_tensor(hw[:, j % 2, :].rearrange("p (e r) -> p e r", e=E),
                                        h_ps[:, 0:ER].rearrange("p (e r) -> p e r", e=E),
                                        gate[:, :].unsqueeze(2).to_broadcast([P, E, R]),
                                        ALU.mult).then_inc(hw_done, 1)
                yield

            def finish(g, j, h):
                n = G * g + j
                dve.wait_ge(ffn_done, 2 * n + h + 1)
                nc.vector.tensor_tensor(x1[:, j, half(h)], out_ps[:, :], x1[:, j, half(h)],
                                        ALU.add).then_inc(out_done, 1)

            for j in range(2):
                feature_stats(0, j, 0)
                feature_stats(0, j, 1)
                feature_stats_in(0, j)
                feature_mean(0, j)
            dve.wait_ge(const_in, 16 * N_CONST)
            dve.wait_ge(tanh_done, 1)
            nc.vector.tensor_scalar(wT[:, :], wT_in[:, :], gates_th[:, 0:1], None, ALU.mult).then_inc(weights_done, 1)
            context_columns(0)
            nc.vector.tensor_scalar(bm[:, :], bm_in[:, :], gates_th[:, 1:2], SCALING, ALU.mult,
                                    ALU.mult).then_inc(weights_done, 1)
            similarities(0)
            dve.wait_ge(setup, 6)
            for _ in split_similarities(0):
                pass
            dve.wait_ge(mean_done, 1)
            nc.vector.tensor_tensor(aT[:, :, :], aT_in[:, :, :],
                                    out_ps[:, 0:ER + E].unsqueeze(1).to_broadcast([P, KC, ER + E]),
                                    ALU.subtract).then_inc(weights_done, 1)

            def body(g, first, last):
                for j in range(G):
                    def before(k):
                        return (g, j - k) if j >= k else (g - 1, j - k + G)
                    one = j >= 1 or not first
                    two = j >= 2 or not first
                    ahead = (g, j + 2) if j < 2 else (g + 1, j - 2)
                    stats = j < 2 or not last
                    gates = gating(*before(1)) if one else iter(())
                    parts = split_similarities(g + 1) if j == 3 and not last else iter(())

                    def steps(of, n):
                        for _ in range(n):
                            next(of, None)

                    modulate(g, j, 0)
                    if one:
                        residual(*before(1), 1)
                    if j == 3 and not last:
                        similarities(g + 1)
                    modulate(g, j, 1)
                    steps(parts, 1)
                    if one:
                        token_stats(*before(1), 1)
                        steps(parts, 1)
                        token_stats_in(*before(1))
                    modulate(g, j, 2)
                    if one:
                        token_variance(*before(1))
                    steps(parts, 1)
                    if two:
                        finish(*before(2), 0)
                    steps(parts, 1)
                    if stats:
                        feature_stats(*ahead, 0)
                    steps(parts, 1)
                    modulate(g, j, 3)
                    if two:
                        finish(*before(2), 1)
                    if stats:
                        feature_stats(*ahead, 1)
                    if j == 2 and not last:
                        context_columns(g + 1)
                    if stats:
                        feature_stats_in(*ahead)
                    residual(g, j, 0)
                    if stats:
                        feature_mean(*ahead)
                    modulate(g, j, 4)
                    steps(gates, 1)
                    if one:
                        logits_in(*before(1))
                    token_stats(g, j, 0)
                    steps(gates, 3)
                    modulate(g, j, 5)
                    steps(gates, 9)

            each_group(dve, body)
            residual(NG - 1, G - 1, 1)
            token_stats(NG - 1, G - 1, 1)
            token_stats_in(NG - 1, G - 1)
            token_variance(NG - 1, G - 1)
            finish(NG - 1, G - 2, 0)
            finish(NG - 1, G - 2, 1)
            gates = gating(NG - 1, G - 1)
            next(gates)
            logits_in(NG - 1, G - 1)
            for _ in gates:
                pass
            finish(NG - 1, G - 1, 0)
            finish(NG - 1, G - 1, 1)

        @block.tensor
        def _(pe):
            def sum_context(g, j):
                pe.wait_ge(sq_done, G * g + j + 1)
                pe.wait_ge(pr_done, G * g + j + 1)
                if j == 0 and not (isinstance(g, int) and g == 0):
                    pe.wait_ge(rows_done, 2 * g)
                for q, src in enumerate((sq, sq, pr, pr)):
                    last = nc.tensor.matmul(sum_ps[32 * q:32 * q + 32, :], onehot[:, j, :],
                                            src[:, j % 2, half(q % 2)], start=(j == 0), stop=(j == G - 1))
                last.then_inc(summed, 1)

            def transpose_context(g):
                pe.wait_ge(sums_out, g + 1)
                for w in range(4):
                    last = nc.tensor.transpose(sum_ps[:, w * P:(w + 1) * P], sums[:, w * P:(w + 1) * P], ident[:, :])
                last.then_inc(ctxT_done, 1)

            def next_norms(g):
                pe.wait_ge(rinv_done, g + 1)
                r = rinv[:, :, :].rearrange("p a b -> p (a b)")
                nc.tensor.matmul(rnext_ps, shifts[:, 0, :], r, start=True, stop=False)
                nc.tensor.matmul(rnext_ps[:, 0:(KC - 1) * G], shifts[:, 1, :], r[:, G:KC * G],
                                 start=False, stop=True).then_inc(rnext_done, 1)

            def transpose_similarities(g):
                pe.wait_ge(split, 5 * (g + 1))
                for c in range(KC):
                    last = nc.tensor.transpose(rows_ps[0:96, c * P:(c + 1) * P],
                                               simp[:, c, :, :].rearrange("p f q -> p (f q)"), identb[:, :])
                last.then_inc(rowsT_done, 1)

            def spread_similarities(g, j, i):
                n = 6 * (G * g + j) + i
                h, k = i // 3, TAP_ORDER[i % 3]
                if i == 0:
                    pe.wait_ge(rows_done, 2 * (g + 1))
                if not (isinstance(g, int) and n < 2):
                    pe.wait_ge(mod_done, n - 1)
                nc.tensor.matmul(sim_ps[i % 2][:, :], sel[:, j, k, :], rows[:, g, half(h)],
                                 start=True, stop=True).then_inc(spread, 1)

            def tap(g, j, i):
                n = 6 * (G * g + j) + i
                h, k = i // 3, TAP_ORDER[i % 3]
                lo = 1 if (k == 0 and h == 0) else 0
                hi = HALF - 1 if (k == 2 and h == 1) else HALF
                if i == 0:
                    pe.wait_ge(wb_done, G * g + j + 1)
                if i % 3 == 0 and not (isinstance(g, int) and g == 0 and j == 0):
                    pe.wait_ge(x1_done, 2 * (G * g + j - 1) + h + 1)
                pe.wait_ge(mod_done, n + 1)
                nc.tensor.matmul(conv_ps[h][:, lo:hi], wb[:, j % 2, k, :], pt[:, (6 * j + i) % 4, lo:hi],
                                 start=(i % 3 == 0), stop=(i % 3 == 2)).then_inc(tap_done, 1)

            def transpose_tokens(g, j, h):
                n = G * g + j
                pe.wait_ge(x1_done, 2 * n + h + 1)
                if not (isinstance(g, int) and n == 0 and h == 0):
                    pe.wait_ge(xT_out, 2 * n + h)
                for c in range(4):
                    last = nc.tensor.transpose(xT_ps[:, c * P:(c + 1) * P],
                                               x1[:, j, h * HALF + c * P:h * HALF + (c + 1) * P], ident[:, :])
                last.then_inc(xT_done, 1)

            def experts_in(g, j, h):
                n = G * g + j
                if h == 0 and not (isinstance(g, int) and n == 0):
                    pe.wait_ge(hwT_out, n)
                pe.wait_ge(xT_out, 2 * n + h + 1)
                for c in range(4 * h, 4 * h + 4):
                    last = nc.tensor.matmul(h_ps, xT[:, j % 2, c, :], aT[:, c, :], start=(c == 0), stop=(c == KC - 1))
                if h == 1:
                    last.then_inc(h_done, 1)

            def transpose_hidden(g, j):
                pe.wait_ge(hw_done, G * g + j + 1)
                nc.tensor.transpose(hwT_ps, hw[:, j % 2, :], ident[:, :]).then_inc(hwT_done, 1)

            def experts_out(g, j, h):
                n = G * g + j
                pe.wait_ge(hwT_out, n + 1)
                if not (isinstance(g, int) and n == 0 and h == 0):
                    pe.wait_ge(out_done, 2 * n + h)
                nc.tensor.matmul(out_ps[:, :], hwT[:, j % 2, :], bm[:, half(h)], start=True,
                                 stop=True).then_inc(ffn_done, 1)

            pe.wait_ge(onehot_in, 16)
            for j in range(G):
                sum_context(0, j)
            pe.wait_ge(const_in, 16 * N_CONST)
            transpose_context(0)
            pe.wait_ge(setup, 6)
            for c in range(KC):
                last = nc.tensor.matmul(out_ps[:, 0:ER + E], mean_w[:, :], aT_in[:, c, :], start=(c == 0),
                                        stop=(c == KC - 1))
            last.then_inc(mean_done, 1)
            next_norms(0)
            transpose_similarities(0)
            spread_similarities(0, 0, 0)
            spread_similarities(0, 0, 1)
            pe.wait_ge(weights_done, 3)

            def body(g, first, last):
                for j in range(G):
                    def before(k):
                        return (g, j - k) if j >= k else (g - 1, j - k + G)
                    one = j >= 1 or not first
                    two = j >= 2 or not first
                    for i in range(6):
                        if i == 1 and two:
                            transpose_hidden(*before(2))
                        if i == 1 and one:
                            transpose_tokens(*before(1), 0)
                        if i == 2 and one:
                            transpose_tokens(*before(1), 1)
                        if i == 2 and two:
                            experts_out(*before(2), 0)
                        if i == 3 and one:
                            experts_in(*before(1), 0)
                        if i == 3 and two:
                            experts_out(*before(2), 1)
                        if i == 4 and one:
                            experts_in(*before(1), 1)
                        if i in (2, 5) and j < 2 and not last:
                            sum_context(g + 1, 2 * j + (i == 5))
                        if i == 3 and j == 2 and not last:
                            transpose_context(g + 1)
                        if i == 5 and j == 2 and not last:
                            next_norms(g + 1)
                        if i == 3 and j == 3 and not last:
                            transpose_similarities(g + 1)
                        tap(g, j, i)
                        if i < 4:
                            spread_similarities(g, j, i + 2)
                        elif j < 3:
                            spread_similarities(g, j + 1, i - 4)
                        elif not last:
                            spread_similarities(g + 1, 0, i - 4)

            each_group(pe, body)
            transpose_hidden(NG - 1, G - 2)
            transpose_tokens(NG - 1, G - 1, 0)
            transpose_tokens(NG - 1, G - 1, 1)
            experts_out(NG - 1, G - 2, 0)
            experts_in(NG - 1, G - 1, 0)
            experts_out(NG - 1, G - 2, 1)
            experts_in(NG - 1, G - 1, 1)
            transpose_hidden(NG - 1, G - 1)
            experts_out(NG - 1, G - 1, 0)
            experts_out(NG - 1, G - 1, 1)



def kernel(x, ctx_4096, g_xattn, g_ffn, L0_xattn_weight, L0_ffn_router_w, L0_ffn_router_b, L0_ffn_A, L0_ffn_Bm):
    import numpy as np
    import concourse.bacc as bacc
    from concourse.bass_utils import run_bass_kernel_spmd

    x, ctx = np.ascontiguousarray(x), np.ascontiguousarray(ctx_4096)
    weight, router_w = np.asarray(L0_xattn_weight), np.asarray(L0_ffn_router_w)
    a, bm = np.asarray(L0_ffn_A), np.asarray(L0_ffn_Bm)
    B, C, T = x.shape
    E, R, _ = a.shape

    conv_wT = np.ascontiguousarray(weight.transpose(1, 2, 0)).reshape(C, TAPS * P)
    rows_a = np.concatenate([a.reshape(E * R, T), router_w], axis=0)
    expert_aT = np.ascontiguousarray(rows_a.T.reshape(T // P, P, E * R + E).transpose(1, 0, 2))
    expert_b = np.ascontiguousarray(bm.transpose(0, 2, 1)).reshape(E * R, T)

    import ml_dtypes
    bf16 = ml_dtypes.bfloat16
    identity = np.eye(P, dtype=np.float32)
    one_hot = np.zeros((P, G, 32), np.float32)
    for b in range(G):
        one_hot[:, b, b] = 1.0
    shift = np.zeros((P, 2, P), np.float32)
    shift[np.arange(1, P), 0, np.arange(P - 1)] = 1.0
    shift[0, 1, P - 1] = 1.0
    select = np.zeros((96, G, TAPS, P), np.float32)
    for c in range(C):
        for k in range(TAPS):
            block = (2, 1, 0)[(c * TAPS + k) // C]
            for part in range(3):
                for b in range(G):
                    select[32 * block + G * part + b, b, k, c] = 1.0
    expert_ids = np.tile(np.arange(E, dtype=np.float32), (P, 1))

    arrays = dict(x=x, ctx=ctx, g_xattn=np.ascontiguousarray(g_xattn), g_ffn=np.ascontiguousarray(g_ffn),
                  conv_wT=conv_wT, expert_aT=expert_aT, router_b=np.ascontiguousarray(L0_ffn_router_b),
                  expert_b=expert_b, identity=identity, identity_bf=identity.astype(bf16), one_hot=one_hot,
                  shift=shift, select=select.astype(bf16), expert_ids=expert_ids)
    nc = bacc.Bacc("TRN2", target_bir_lowering=False, num_devices=1)
    ins = {n: nc.dram_tensor(n, v.shape, mybir.dt.from_np(v.dtype), kind="ExternalInput").ap()
           for n, v in arrays.items()}
    out = nc.dram_tensor("out", x.shape, F32, kind="ExternalOutput").ap()
    flamingo_kernel(nc, **ins, out=out)
    r = run_bass_kernel_spmd(nc, [arrays], core_ids=[0])
    return r.results[0]["out"]
```

```python
import concourse.bass as bass
from concourse import mybir
from contextlib import ExitStack

F32 = mybir.dt.float32
F32R = mybir.dt.float32r
BF16 = mybir.dt.bfloat16
U32 = mybir.dt.uint32
ALU = mybir.AluOpType
ACT = mybir.ActivationFunctionType

P = 128
HALF = 512
LN_EPS = 1e-5
COS_EPS = 1e-8
TAPS = 3
G = 4
TAP_ORDER = (1, 0, 2)


def flamingo_kernel(nc, x, ctx, g_xattn, g_ffn, conv_wT, expert_aT, router_b, expert_b,
                    identity, identity_bf, one_hot, shift, select, expert_ids, out):
    B, C, T = x.shape
    NG = B // G
    KC = T // P
    E = router_b.shape[0]
    ER = expert_aT.shape[2] - E
    R = ER // E
    SCALING = 8.0 / R
    assert C == P and T == 2 * HALF and ER == P and B % G == 0 and NG >= 3

    st = ExitStack()
    with st:
        def sb(name, shape, dt=F32):
            return st.enter_context(nc.sbuf_tensor(name, shape, dt))

        def sem(name):
            return st.enter_context(nc.semaphore(name))

        ident = sb("ident", [P, P])
        identb = sb("identb", [P, P], BF16)
        onehot = sb("onehot", [P, G, 32])
        shifts = sb("shifts", [P, 2, P])
        sel = sb("sel", [96, G, TAPS, P], BF16)
        ids = sb("ids", [P, E])
        mean_w = sb("mean_w", [P, P])
        minus_half = sb("minus_half", [P, KC * G])
        eps = sb("eps", [P, 1])
        gates_in = sb("gates_in", [P, 2])
        gates_th = sb("gates_th", [P, 2])
        wT_in = sb("wT_in", [P, TAPS * P])
        wT = sb("wT", [P, TAPS * P])
        aT_in = sb("aT_in", [P, KC, ER + E])
        aT = sb("aT", [P, KC, ER + E])
        rb = sb("rb", [P, E])
        bm_in = sb("bm_in", [P, T])
        bm = sb("bm", [P, T])
        bm_hi = sb("bm_hi", [P, T], F32R)
        bm_lo = sb("bm_lo", [P, T], F32R)
        et = sb("et", [P, G, T])
        sq = sb("sq", [P, 2, T])
        pr = sb("pr", [P, 2, T])
        sums = sb("sums", [P, HALF])
        nd = sb("nd", [P, 4, G, G])
        nmax = sb("nmax", [P, KC, G])
        rinv = sb("rinv", [P, KC, G])
        dr = sb("dr", [P, KC, G])
        nr = sb("nr", [P, KC, G])
        sim = sb("sim", [P, KC, 3, G])
        rest1 = sb("rest1", [P, KC, 3, G])
        rest2 = sb("rest2", [P, KC, 3, G])
        simp = sb("simp", [P, KC, 3, 32], BF16)
        rows = sb("rows", [96, NG, T], BF16)
        xt = sb("xt", [P, G, T])
        x1 = sb("x1", [P, G, T])
        bn1 = sb("bn1", [P, 2, 12])
        mv1 = sb("mv1", [P, G, 2])
        ve1 = sb("ve1", [P, G])
        rs1 = sb("rs1", [P, G])
        wb = sb("wb", [P, 2, TAPS, P])
        pt = sb("pt", [P, 4, HALF])
        bn2 = sb("bn2", [P, 2, 12])
        mv2 = sb("mv2", [P, 2, 2])
        ve2 = sb("ve2", [P, 2])
        rs2 = sb("rs2", [P, 2])
        xT = sb("xT", [P, 2, KC, P])
        logit = sb("logit", [P, E])
        top = sb("top", [P, 8])
        topi = sb("topi", [P, 8], U32)
        below = sb("below", [P, E])
        expo = sb("expo", [P, E])
        pick0 = sb("pick0", [P, E])
        pick = sb("pick", [P, E])
        expk = sb("expk", [P, E])
        esum = sb("esum", [P, 1])
        einv = sb("einv", [P, 1])
        gate = sb("gate", [P, E])
        hw = sb("hw", [P, 2, ER])
        hs = sb("hs", [P, 2, ER + E])
        hwT = sb("hwT", [P, 2, P])
        hwT_hi = sb("hwT_hi", [P, 2, P], F32R)
        hwT_lo = sb("hwT_lo", [P, 2, P], F32R)

        bank = [st.enter_context(nc.psum_tensor(f"bank{i}", [P, HALF], F32)) for i in range(8)]
        sim_ps = bank[0:2]
        conv_ps = bank[2:4]
        xT_ps = bank[4]
        out_ps = bank[5]
        h_ps = bank[6][:, 0:ER + E]
        hwT_ps = bank[6][:, 256:256 + P]
        sum_ps = bank[7]
        ctxT_ps = bank[7][:, :].rearrange("p (w q b) -> p q w b", w=4, q=4)
        rnext_ps = bank[7][:, 0:KC * G]
        rows_ps = bank[7][:, :].bitcast(BF16)

        const_in = sem("const_in")
        onehot_in = sem("onehot_in")
        e_in = [sem(f"e_in{j}") for j in range(G)]
        x_in = [sem(f"x_in{j}") for j in range(G)]
        stored = [sem(f"stored{j}") for j in range(G)]
        setup = sem("setup")
        tanh_done = sem("tanh_done")
        mean_done = sem("mean_done")
        weights_done = sem("weights_done")
        sq_done = sem("sq_done")
        pr_done = sem("pr_done")
        summed = sem("summed")
        sums_out = sem("sums_out")
        ctxT_done = sem("ctxT_done")
        nd_done = sem("nd_done")
        nmax_done = sem("nmax_done")
        rinv_done = sem("rinv_done")
        rnext_done = sem("rnext_done")
        partial = sem("partial")
        sim_done = sem("sim_done")
        split = sem("split")
        rowsT_done = sem("rowsT_done")
        rows_done = sem("rows_done")
        bn1_done = sem("bn1_done")
        mv1_done = sem("mv1_done")
        ve1_done = sem("ve1_done")
        rs1_done = sem("rs1_done")
        wb_done = sem("wb_done")
        spread = sem("spread")
        mod_done = sem("mod_done")
        tap_done = sem("tap_done")
        x1_done = sem("x1_done")
        bn2_done = sem("bn2_done")
        mv2_done = sem("mv2_done")
        ve2_done = sem("ve2_done")
        rs2_done = sem("rs2_done")
        xT_done = sem("xT_done")
        xT_out = sem("xT_out")
        h_done = sem("h_done")
        h_out = sem("h_out")
        logit_done = sem("logit_done")
        top_done = sem("top_done")
        topi_done = sem("topi_done")
        below_done = sem("below_done")
        expo_done = sem("expo_done")
        pick0_done = sem("pick0_done")
        pick_done = sem("pick_done")
        esum_done = sem("esum_done")
        einv_done = sem("einv_done")
        gate_done = sem("gate_done")
        hw_done = sem("hw_done")
        hwT_done = sem("hwT_done")
        hwT_out = sem("hwT_out")
        hwT_rest = sem("hwT_rest")
        ffn_done = sem("ffn_done")
        out_done = sem("out_done")
        N_CONST = 11

        block = st.enter_context(nc.Block())

        def each_group(eng, body):
            body(0, True, False)
            with eng.Fori(1, NG - 1) as g:
                body(g, False, False)
            body(NG - 1, False, True)

        def past(g, j, k):
            return not isinstance(g, int) or G * g + j >= k

        def half(h):
            return slice(h * HALF, (h + 1) * HALF)

        @block.sync
        def _(sp):
            def load_e(g, j):
                if past(g, 0, 1):
                    sp.wait_ge(sq_done, G * g + j - G + 1)
                    sp.wait_ge(pr_done, G * g + j - G + 1)
                sp.dma_start(et[:, j, :], ctx[G * g + j, :, :]).then_inc(e_in[j], 16)

            def load_x(g, j):
                if past(g, 0, 1):
                    sp.wait_ge(x1_done, 2 * (G * g + j - G + 1))
                sp.dma_start(xt[:, j, :], x[G * g + j, :, :]).then_inc(x_in[j], 16)

            def store(g, j):
                sp.wait_ge(out_done, 2 * (G * g + j + 1))
                sp.dma_start(out[G * g + j, :, :], x1[:, j, :]).then_inc(stored[j], 16)

            load_e(0, 0)
            load_e(0, 1)
            sp.dma_start(onehot[:, :, :], one_hot).then_inc(onehot_in, 16)
            load_e(0, 2)
            load_e(0, 3)
            sp.dma_start(ident[:, :], identity).then_inc(const_in, 16)
            load_x(0, 0)
            sp.dma_start(identb[:, :], identity_bf).then_inc(const_in, 16)
            sp.dma_start(shifts[:, :, :], shift).then_inc(const_in, 16)
            sp.dma_start(sel[:, :, :, :], select).then_inc(const_in, 16)
            sp.dma_start(wT_in[:, :], conv_wT).then_inc(const_in, 16)
            sp.dma_start(gates_in[:, 0:1], g_xattn.rearrange("(a n) -> a n", a=1).to_broadcast([P, 1])).then_inc(const_in, 16)
            sp.dma_start(gates_in[:, 1:2], g_ffn.rearrange("(a n) -> a n", a=1).to_broadcast([P, 1])).then_inc(const_in, 16)
            sp.dma_start(ids[:, :], expert_ids).then_inc(const_in, 16)
            sp.dma_start(rb[:, :], router_b.rearrange("(a n) -> a n", a=1).to_broadcast([P, E])).then_inc(const_in, 16)
            sp.dma_start(aT_in[:, :, :], expert_aT).then_inc(const_in, 16)
            load_x(0, 1)
            load_x(0, 2)
            sp.dma_start(bm_in[:, :], expert_b).then_inc(const_in, 16)
            for j in range(G):
                load_e(1, j)
            load_x(0, 3)

            def body(g, first, last):
                for j in range(G):
                    if j > 0 and not last:
                        load_x(g + 1, j - 1)
                    if j == 0 and not first:
                        load_x(g, G - 1)
                    if j == 1 and not last and not (isinstance(g, int) and g + 2 >= NG):
                        load_e(g + 2, 0)
                        load_e(g + 2, 1)
                    if j == 2 and not last and not (isinstance(g, int) and g + 2 >= NG):
                        load_e(g + 2, 2)
                        load_e(g + 2, 3)
                    if j >= 3:
                        store(g, j - 3)
                    elif not first:
                        store(g - 1, j + 1)

            body(0, True, False)
            with sp.Fori(1, NG - 2) as g:
                body(g, False, False)
            body(NG - 2, False, False)
            body(NG - 1, False, True)
            for j in range(1, G):
                store(NG - 1, j)
            for j in range(G):
                sp.wait_ge(stored[j], 16 * NG)

        @block.gpsimd
        def _(pool):
            nc.gpsimd.memset(eps[:, :], LN_EPS).then_inc(setup, 1)
            nc.gpsimd.memset(minus_half[:, :], -0.5).then_inc(setup, 1)
            nc.gpsimd.memset(mean_w[:, :], 1.0 / T).then_inc(setup, 1)
            nc.gpsimd.memset(pr[:, :, T - 1:T], 0.0).then_inc(setup, 1)
            nc.gpsimd.memset(simp[:, :, :, :], 0.0).then_inc(setup, 1)
            nc.gpsimd.memset(rows[:, :, :], 0.0).then_inc(setup, 1)
            pool.wait_ge(setup, 6)

            def product(g, j):
                if past(g, j, 2):
                    pool.wait_ge(summed, G * g + j - 1)
                pool.wait_ge(e_in[j], 16 * (g + 1))
                nc.gpsimd.tensor_tensor(pr[:, j % 2, 0:T - 1], et[:, j, 0:T - 1], et[:, j, 1:T],
                                        ALU.mult).then_inc(pr_done, 1)

            def inverse_norms(g):
                pool.wait_ge(nmax_done, g + 1)
                nc.gpsimd.tensor_tensor(rinv[:, :, :].rearrange("p a b -> p (a b)"),
                                        nmax[:, :, :].rearrange("p a b -> p (a b)"),
                                        minus_half[:, :], ALU.pow).then_inc(rinv_done, 1)

            def feature_rstd(g, j):
                pool.wait_ge(mv1_done, G * g + j + 1)
                nc.gpsimd.tensor_tensor(ve1[:, j:j + 1], mv1[:, j, 1:2], eps[:, :], ALU.add).then_inc(ve1_done, 1)
                pool.wait_ge(ve1_done, G * g + j + 1)
                nc.gpsimd.tensor_tensor(rs1[:, j:j + 1], ve1[:, j:j + 1], minus_half[:, 0:1],
                                        ALU.pow).then_inc(rs1_done, 1)

            def hidden(g, j):
                i, n = j % 2, G * g + j
                pool.wait_ge(gate_done, n + 1)
                if past(g, j, 2):
                    pool.wait_ge(hwT_done, n - 1)
                nc.gpsimd.tensor_tensor(hw[:, i, :].rearrange("p (e r) -> p e r", e=E),
                                        hs[:, i, 0:ER].rearrange("p (e r) -> p e r", e=E),
                                        gate[:, :].unsqueeze(2).to_broadcast([P, E, R]),
                                        ALU.mult).then_inc(hw_done, 1)

            def hidden_rest(g, j):
                i, n = j % 2, G * g + j
                pool.wait_ge(hwT_out, 2 * (n + 1))
                if past(g, j, 2):
                    pool.wait_ge(ffn_done, 2 * (n - 1))
                nc.gpsimd.tensor_tensor(hwT_lo[:, i, :], hwT[:, i, :], hwT_hi[:, i, :],
                                        ALU.subtract).then_inc(hwT_rest, 1)

            def token_rstd(g, j):
                i = j % 2
                pool.wait_ge(mv2_done, G * g + j + 1)
                nc.gpsimd.tensor_tensor(ve2[:, i:i + 1], mv2[:, i, 1:2], eps[:, :], ALU.add).then_inc(ve2_done, 1)
                pool.wait_ge(ve2_done, G * g + j + 1)
                nc.gpsimd.tensor_tensor(rs2[:, i:i + 1], ve2[:, i:i + 1], minus_half[:, 0:1],
                                        ALU.pow).then_inc(rs2_done, 1)

            for j in range(G):
                product(0, j)
            inverse_norms(0)
            feature_rstd(0, 0)
            feature_rstd(0, 1)

            def body(g, first, last):
                for j in range(G):
                    def before(k):
                        return (g, j - k) if j >= k else (g - 1, j - k + G)
                    one = j >= 1 or not first
                    two = j >= 2 or not first
                    if j < 2 and not last:
                        product(g + 1, 2 * j)
                    if two:
                        hidden(*before(2))
                    if one:
                        token_rstd(*before(1))
                    if two:
                        hidden_rest(*before(2))
                    if j < 2 and not last:
                        product(g + 1, 2 * j + 1)
                    if j == 2 and not last:
                        inverse_norms(g + 1)
                    if j < 2:
                        feature_rstd(g, j + 2)
                    elif not last:
                        feature_rstd(g + 1, j - 2)

            each_group(pool, body)
            hidden(NG - 1, G - 2)
            token_rstd(NG - 1, G - 1)
            hidden_rest(NG - 1, G - 2)
            hidden(NG - 1, G - 1)
            hidden_rest(NG - 1, G - 1)

        @block.scalar
        def _(act):
            def square(g, j):
                if past(g, j, 2):
                    act.wait_ge(summed, G * g + j - 1)
                act.wait_ge(e_in[j], 16 * (g + 1))
                nc.scalar.activation(sq[:, j % 2, :], et[:, j, :], ACT.Square).then_inc(sq_done, 1)

            def sums_evacuate(g):
                act.wait_ge(summed, G * (g + 1))
                if past(g, 0, 1):
                    act.wait_ge(ctxT_done, g)
                nc.scalar.activation(sums[:, :], sum_ps[:, :], ACT.Copy).then_inc(sums_out, 1)

            def rows_evacuate(g):
                act.wait_ge(rowsT_done, g + 1)
                nc.scalar.activation(rows[64:96, g, 1:T], rows_ps[64:96, 0:T - 1], ACT.Copy).then_inc(rows_done, 1)
                nc.scalar.activation(rows[0:64, g, :], rows_ps[0:64, :], ACT.Copy).then_inc(rows_done, 1)

            def scale_weights(g, j):
                act.wait_ge(rs1_done, G * g + j + 1)
                if past(g, j, 2):
                    act.wait_ge(tap_done, 6 * (G * g + j - 1))
                nc.scalar.activation(wb[:, j % 2, :, :].rearrange("p k o -> p (k o)"), wT[:, :], ACT.Copy,
                                     scale=rs1[:, j:j + 1]).then_inc(wb_done, 1)

            def tokens_evacuate(g, j, h):
                act.wait_ge(xT_done, 2 * (G * g + j) + h + 1)
                if past(g, j, 2):
                    act.wait_ge(h_done, G * g + j - 1)
                nc.scalar.activation(xT[:, j % 2, 4 * h:4 * h + 4, :].rearrange("p c n -> p (c n)"),
                                     xT_ps[:, :], ACT.Copy).then_inc(xT_out, 1)

            def exponent(g, j):
                act.wait_ge(below_done, G * g + j + 1)
                if past(g, j, 1):
                    act.wait_ge(esum_done, G * g + j)
                nc.scalar.activation(expo[:, :], below[:, :], ACT.Exp).then_inc(expo_done, 1)

            def logits_evacuate(g, j):
                n = G * g + j
                act.wait_ge(h_done, n + 1)
                if past(g, j, 2):
                    act.wait_ge(hw_done, n - 1)
                nc.scalar.activation(hs[:, j % 2, :], h_ps, ACT.Copy).then_inc(h_out, 1)

            def hidden_evacuate(g, j):
                i, n = j % 2, G * g + j
                act.wait_ge(hwT_done, n + 1)
                if past(g, j, 2):
                    act.wait_ge(ffn_done, 2 * (n - 1))
                nc.scalar.activation(hwT[:, i, :], hwT_ps, ACT.Copy).then_inc(hwT_out, 1)
                nc.scalar.activation(hwT_hi[:, i, :], hwT_ps, ACT.Copy).then_inc(hwT_out, 1)

            square(0, 0)
            square(0, 1)
            square(0, 2)
            square(0, 3)
            act.wait_ge(const_in, 16 * N_CONST)
            nc.scalar.activation(gates_th[:, :], gates_in[:, :], ACT.Tanh).then_inc(tanh_done, 1)
            sums_evacuate(0)
            act.wait_ge(weights_done, 1)
            scale_weights(0, 0)
            act.wait_ge(setup, 6)
            rows_evacuate(0)

            def body(g, first, last):
                for j in range(G):
                    def before(k):
                        return (g, j - k) if j >= k else (g - 1, j - k + G)
                    one = j >= 1 or not first
                    two = j >= 2 or not first
                    if j < 2 and not last:
                        square(g + 1, 2 * j)
                    if j == 2 and not last:
                        sums_evacuate(g + 1)
                    if one:
                        tokens_evacuate(*before(1), 1)
                        logits_evacuate(*before(1))
                    if j == 3 and not last:
                        rows_evacuate(g + 1)
                    if two:
                        hidden_evacuate(*before(2))
                    if j < 3:
                        scale_weights(g, j + 1)
                    elif not last:
                        scale_weights(g + 1, 0)
                    if j < 2 and not last:
                        square(g + 1, 2 * j + 1)
                    if one:
                        exponent(*before(1))
                    tokens_evacuate(g, j, 0)

            each_group(act, body)
            tokens_evacuate(NG - 1, G - 1, 1)
            logits_evacuate(NG - 1, G - 1)
            hidden_evacuate(NG - 1, G - 2)
            exponent(NG - 1, G - 1)
            hidden_evacuate(NG - 1, G - 1)

        @block.vector
        def _(dve):
            def feature_stats(g, j, h):
                if h == 0:
                    dve.wait_ge(x_in[j], 16 * (g + 1))
                nc.vector.bn_stats(bn1[:, j % 2, 6 * h:6 * h + 6], xt[:, j, half(h)]).then_inc(bn1_done, 1)

            def feature_stats_in(g, j):
                dve.wait_ge(bn1_done, 2 * (G * g + j + 1))
                if past(g, 0, 1):
                    dve.wait_ge(rs1_done, G * g + j - G + 1)

            def feature_mean(g, j):
                nc.vector.bn_aggr(mv1[:, j, :], bn1[:, j % 2, :]).then_inc(mv1_done, 1)

            def context_columns(g):
                dve.wait_ge(ctxT_done, g + 1)
                nc.vector.tensor_copy(nd[:, :, :, :], ctxT_ps[:, :, :, 0:G]).then_inc(nd_done, 1)
                dve.wait_ge(nd_done, g + 1)
                nc.vector.tensor_scalar(nmax[:, :, :].rearrange("p a b -> p (a b)"),
                                        nd[:, 0:2, :, :].rearrange("p h w b -> p (h w b)"),
                                        COS_EPS * COS_EPS, None, ALU.max).then_inc(nmax_done, 1)

            norms = nd[:, 0:2, :, :].rearrange("p h w b -> p (h w) b")
            dots = nd[:, 2:4, :, :].rearrange("p h w b -> p (h w) b")

            def similarities(g):
                dve.wait_ge(rinv_done, g + 1)
                nc.vector.tensor_tensor(dr[:, :, :], dots, rinv[:, :, :], ALU.mult).then_inc(partial, 1)
                nc.vector.tensor_tensor(nr[:, :, :], norms, rinv[:, :, :], ALU.mult).then_inc(partial, 1)
                dve.wait_ge(rnext_done, g + 1)
                dve.wait_ge(partial, 2 * (g + 1))
                nc.vector.tensor_tensor(sim[:, :, 0:3:2, :],
                                        dr[:, :, :].unsqueeze(2).to_broadcast([P, KC, 2, G]),
                                        rnext_ps.rearrange("p (a b) -> p a b", b=G).unsqueeze(2).to_broadcast([P, KC, 2, G]),
                                        ALU.mult).then_inc(sim_done, 1)
                nc.vector.tensor_tensor(sim[:, :, 1, :], nr[:, :, :], rinv[:, :, :], ALU.mult).then_inc(sim_done, 1)

            def split_similarities(g):
                part = [simp[:, :, :, G * i:G * i + G] for i in range(3)]
                dve.wait_ge(sim_done, 2 * (g + 1))
                nc.vector.tensor_copy(part[0], sim[:, :, :, :]).then_inc(split, 1)
                yield
                dve.wait_ge(split, 5 * g + 1)
                nc.vector.tensor_tensor(rest1[:, :, :, :], sim[:, :, :, :], part[0], ALU.subtract).then_inc(split, 1)
                yield
                dve.wait_ge(split, 5 * g + 2)
                nc.vector.tensor_copy(part[1], rest1[:, :, :, :]).then_inc(split, 1)
                yield
                dve.wait_ge(split, 5 * g + 3)
                nc.vector.tensor_tensor(rest2[:, :, :, :], rest1[:, :, :, :], part[1], ALU.subtract).then_inc(split, 1)
                yield
                dve.wait_ge(split, 5 * g + 4)
                nc.vector.tensor_copy(part[2], rest2[:, :, :, :]).then_inc(split, 1)
                yield

            def modulate(g, j, i):
                n = 6 * (G * g + j) + i
                h, k = i // 3, TAP_ORDER[i % 3]
                lo = 1 if (k == 0 and h == 0) else 0
                hi = HALF - 1 if (k == 2 and h == 1) else HALF
                c = h * HALF + k - 1
                dve.wait_ge(spread, n + 1)
                if not (isinstance(g, int) and n < 4):
                    dve.wait_ge(tap_done, n - 3)
                nc.vector.scalar_tensor_tensor(
                    out=pt[:, (6 * j + i) % 4, lo:hi],
                    in0=xt[:, j, c + lo:c + hi], scalar=mv1[:, j, 0:1], in1=sim_ps[i % 2][:, lo:hi],
                    op0=ALU.subtract, op1=ALU.mult).then_inc(mod_done, 1)

            def residual(g, j, h):
                n = G * g + j
                dve.wait_ge(tap_done, 6 * n + 3 * (h + 1))
                if h == 0 and not (isinstance(g, int) and g == 0):
                    dve.wait_ge(stored[j], 16 * g)
                nc.vector.tensor_tensor(x1[:, j, half(h)], conv_ps[h][:, :], xt[:, j, half(h)],
                                        ALU.add).then_inc(x1_done, 1)

            def token_stats(g, j, h):
                n = G * g + j
                dve.wait_ge(x1_done, 2 * n + h + 1)
                nc.vector.bn_stats(bn2[:, j % 2, 6 * h:6 * h + 6], x1[:, j, half(h)]).then_inc(bn2_done, 1)

            def token_stats_in(g, j):
                dve.wait_ge(bn2_done, 2 * (G * g + j + 1))

            def logits_in(g, j):
                dve.wait_ge(logit_done, G * g + j + 1)

            def token_variance(g, j):
                nc.vector.bn_aggr(mv2[:, j % 2, :], bn2[:, j % 2, :]).then_inc(mv2_done, 1)

            def pick_experts(g, j):
                n = G * g + j
                dve.wait_ge(rs2_done, n + 1)
                dve.wait_ge(h_out, n + 1)
                nc.vector.scalar_tensor_tensor(out=logit[:, :], in0=hs[:, j % 2, ER:ER + E],
                                               scalar=rs2[:, j % 2:j % 2 + 1], in1=rb[:, :],
                                               op0=ALU.mult, op1=ALU.add).then_inc(logit_done, 1)
                yield
                nc.vector.max(top[:, :], logit[:, :]).then_inc(top_done, 1)
                yield
                dve.wait_ge(top_done, n + 1)
                nc.vector.tensor_scalar(below[:, :], logit[:, :], top[:, 0:1], None, ALU.subtract).then_inc(below_done, 1)
                nc.vector.max_index(topi[:, :], top[:, :], logit[:, :]).then_inc(topi_done, 1)
                yield

            def weigh_experts(g, j):
                n = G * g + j
                dve.wait_ge(topi_done, n + 1)
                nc.vector.tensor_scalar(pick0[:, :], ids[:, :], topi[:, 0:1], None, ALU.is_equal).then_inc(pick0_done, 1)
                yield
                dve.wait_ge(pick0_done, n + 1)
                nc.vector.scalar_tensor_tensor(out=pick[:, :], in0=ids[:, :], scalar=topi[:, 1:2], in1=pick0[:, :],
                                               op0=ALU.is_equal, op1=ALU.add).then_inc(pick_done, 1)
                yield

                dve.wait_ge(pick_done, n + 1)
                dve.wait_ge(expo_done, n + 1)
                nc.vector.scalar_tensor_tensor(out=expk[:, :], in0=expo[:, :], scalar=1.0, in1=pick[:, :],
                                               op0=ALU.mult, op1=ALU.mult, accum_out=esum[:, :]).then_inc(esum_done, 1)
                yield
                dve.wait_ge(esum_done, n + 1)
                nc.vector.reciprocal(einv[:, :], esum[:, :]).then_inc(einv_done, 1)
                yield
                dve.wait_ge(einv_done, n + 1)
                if past(g, j, 1):
                    dve.wait_ge(hw_done, n)
                nc.vector.tensor_scalar(gate[:, :], expk[:, :], einv[:, :], rs2[:, j % 2:j % 2 + 1], ALU.mult,
                                        ALU.mult).then_inc(gate_done, 1)
                yield

            def finish(g, j, h):
                n = G * g + j
                dve.wait_ge(ffn_done, 2 * n + h + 1)
                nc.vector.tensor_tensor(x1[:, j, half(h)], out_ps[:, :], x1[:, j, half(h)],
                                        ALU.add).then_inc(out_done, 1)

            for j in range(2):
                feature_stats(0, j, 0)
                feature_stats(0, j, 1)
                feature_stats_in(0, j)
                feature_mean(0, j)
            dve.wait_ge(const_in, 16 * N_CONST)
            dve.wait_ge(tanh_done, 1)
            nc.vector.tensor_scalar(wT[:, :], wT_in[:, :], gates_th[:, 0:1], None, ALU.mult).then_inc(weights_done, 1)
            context_columns(0)
            nc.vector.tensor_scalar(bm[:, :], bm_in[:, :], gates_th[:, 1:2], SCALING, ALU.mult,
                                    ALU.mult).then_inc(weights_done, 1)
            dve.wait_ge(weights_done, 2)
            nc.vector.tensor_copy(bm_hi[:, :], bm[:, :]).then_inc(weights_done, 1)
            similarities(0)
            dve.wait_ge(weights_done, 3)
            nc.vector.tensor_tensor(bm_lo[:, :], bm[:, :], bm_hi[:, :], ALU.subtract).then_inc(weights_done, 1)
            dve.wait_ge(setup, 6)
            for _ in split_similarities(0):
                pass
            dve.wait_ge(mean_done, 1)
            nc.vector.tensor_tensor(aT[:, :, :], aT_in[:, :, :],
                                    out_ps[:, 0:ER + E].unsqueeze(1).to_broadcast([P, KC, ER + E]),
                                    ALU.subtract).then_inc(weights_done, 1)

            def body(g, first, last):
                for j in range(G):
                    def before(k):
                        return (g, j - k) if j >= k else (g - 1, j - k + G)
                    one = j >= 1 or not first
                    two = j >= 2 or not first
                    three = j >= 3 or not first
                    ahead = (g, j + 2) if j < 2 else (g + 1, j - 2)
                    stats = j < 2 or not last
                    nothing = iter(())
                    picks = pick_experts(*before(1)) if one else nothing
                    weights = weigh_experts(*before(2)) if two else nothing
                    parts = split_similarities(g + 1) if j == 3 and not last else nothing

                    def steps(of, n=1):
                        for _ in range(n):
                            next(of, None)

                    modulate(g, j, 0)
                    steps(weights)
                    if three:
                        finish(*before(3), 0)
                    steps(weights)
                    modulate(g, j, 1)
                    steps(weights)
                    if three:
                        finish(*before(3), 1)
                    steps(weights)
                    if one:
                        residual(*before(1), 1)
                    steps(weights)
                    if j == 3 and not last:
                        similarities(g + 1)
                    modulate(g, j, 2)
                    steps(parts)
                    if one:
                        token_stats(*before(1), 1)
                        steps(parts)
                        token_stats_in(*before(1))
                    modulate(g, j, 3)
                    if one:
                        token_variance(*before(1))
                    steps(parts)
                    if stats:
                        feature_stats(*ahead, 0)
                    steps(parts)
                    modulate(g, j, 4)
                    steps(parts)
                    steps(picks)
                    if one:
                        logits_in(*before(1))
                    residual(g, j, 0)
                    if j == 2 and not last:
                        context_columns(g + 1)
                    steps(picks)
                    if stats:
                        feature_stats(*ahead, 1)
                        feature_stats_in(*ahead)
                    modulate(g, j, 5)
                    if stats:
                        feature_mean(*ahead)
                    steps(picks)
                    token_stats(g, j, 0)

            each_group(dve, body)
            weights = weigh_experts(NG - 1, G - 2)
            next(weights)
            finish(NG - 1, G - 3, 0)
            next(weights)
            residual(NG - 1, G - 1, 1)
            next(weights)
            token_stats(NG - 1, G - 1, 1)
            next(weights)
            finish(NG - 1, G - 3, 1)
            next(weights)
            token_stats_in(NG - 1, G - 1)
            token_variance(NG - 1, G - 1)
            picks = pick_experts(NG - 1, G - 1)
            next(picks)
            logits_in(NG - 1, G - 1)
            for _ in picks:
                pass
            finish(NG - 1, G - 2, 0)
            for _ in weigh_experts(NG - 1, G - 1):
                pass
            finish(NG - 1, G - 2, 1)
            finish(NG - 1, G - 1, 0)
            finish(NG - 1, G - 1, 1)

        @block.tensor
        def _(pe):
            def sum_context(g, j):
                pe.wait_ge(sq_done, G * g + j + 1)
                pe.wait_ge(pr_done, G * g + j + 1)
                if j == 0 and not (isinstance(g, int) and g == 0):
                    pe.wait_ge(rows_done, 2 * g)
                for q, src in enumerate((sq, sq, pr, pr)):
                    last = nc.tensor.matmul(sum_ps[32 * q:32 * q + 32, :], onehot[:, j, :],
                                            src[:, j % 2, half(q % 2)], start=(j == 0), stop=(j == G - 1))
                last.then_inc(summed, 1)

            def transpose_context(g):
                pe.wait_ge(sums_out, g + 1)
                for w in range(4):
                    last = nc.tensor.transpose(sum_ps[:, w * P:(w + 1) * P], sums[:, w * P:(w + 1) * P], ident[:, :])
                last.then_inc(ctxT_done, 1)

            def next_norms(g):
                pe.wait_ge(rinv_done, g + 1)
                r = rinv[:, :, :].rearrange("p a b -> p (a b)")
                nc.tensor.matmul(rnext_ps, shifts[:, 0, :], r, start=True, stop=False)
                nc.tensor.matmul(rnext_ps[:, 0:(KC - 1) * G], shifts[:, 1, :], r[:, G:KC * G],
                                 start=False, stop=True).then_inc(rnext_done, 1)

            def transpose_similarities(g):
                pe.wait_ge(split, 5 * (g + 1))
                for c in range(KC):
                    last = nc.tensor.transpose(rows_ps[0:96, c * P:(c + 1) * P],
                                               simp[:, c, :, :].rearrange("p f q -> p (f q)"), identb[:, :])
                last.then_inc(rowsT_done, 1)

            def spread_similarities(g, j, i):
                n = 6 * (G * g + j) + i
                h, k = i // 3, TAP_ORDER[i % 3]
                if i == 0:
                    pe.wait_ge(rows_done, 2 * (g + 1))
                if not (isinstance(g, int) and n < 2):
                    pe.wait_ge(mod_done, n - 1)
                nc.tensor.matmul(sim_ps[i % 2][:, :], sel[:, j, k, :], rows[:, g, half(h)],
                                 start=True, stop=True).then_inc(spread, 1)

            def tap(g, j, i):
                n = 6 * (G * g + j) + i
                h, k = i // 3, TAP_ORDER[i % 3]
                lo = 1 if (k == 0 and h == 0) else 0
                hi = HALF - 1 if (k == 2 and h == 1) else HALF
                if i == 0:
                    pe.wait_ge(wb_done, G * g + j + 1)
                if i % 3 == 0 and not (isinstance(g, int) and g == 0 and j == 0):
                    pe.wait_ge(x1_done, 2 * (G * g + j - 1) + h + 1)
                pe.wait_ge(mod_done, n + 1)
                nc.tensor.matmul(conv_ps[h][:, lo:hi], wb[:, j % 2, k, :], pt[:, (6 * j + i) % 4, lo:hi],
                                 start=(i % 3 == 0), stop=(i % 3 == 2)).then_inc(tap_done, 1)

            def transpose_tokens(g, j, h):
                n = G * g + j
                pe.wait_ge(x1_done, 2 * n + h + 1)
                if not (isinstance(g, int) and n == 0 and h == 0):
                    pe.wait_ge(xT_out, 2 * n + h)
                for c in range(4):
                    last = nc.tensor.transpose(xT_ps[:, c * P:(c + 1) * P],
                                               x1[:, j, h * HALF + c * P:h * HALF + (c + 1) * P], ident[:, :])
                last.then_inc(xT_done, 1)

            def experts_in(g, j, h):
                n = G * g + j
                if h == 0 and past(g, j, 1):
                    pe.wait_ge(h_out, n)
                    if past(g, j, 2):
                        pe.wait_ge(hwT_out, 2 * (n - 1))
                pe.wait_ge(xT_out, 2 * n + h + 1)
                for c in range(4 * h, 4 * h + 4):
                    last = nc.tensor.matmul(h_ps, xT[:, j % 2, c, :], aT[:, c, :], start=(c == 0), stop=(c == KC - 1))
                if h == 1:
                    last.then_inc(h_done, 1)

            def transpose_hidden(g, j, newest):
                pe.wait_ge(hw_done, G * g + j + 1)
                pe.wait_ge(h_out, newest + 1)
                nc.tensor.transpose(hwT_ps, hw[:, j % 2, :], ident[:, :]).then_inc(hwT_done, 1)

            def experts_out(g, j, h):
                n = G * g + j
                pe.wait_ge(hwT_rest, n + 1)
                if not (isinstance(g, int) and n == 0 and h == 0):
                    pe.wait_ge(out_done, 2 * n + h)
                hi, lo = hwT_hi[:, j % 2, :], hwT_lo[:, j % 2, :]
                nc.tensor.matmul(out_ps[:, :], hi, bm_hi[:, half(h)], start=True, stop=False)
                nc.tensor.matmul(out_ps[:, :], hi, bm_lo[:, half(h)], start=False, stop=False)
                nc.tensor.matmul(out_ps[:, :], lo, bm_hi[:, half(h)], start=False, stop=True).then_inc(ffn_done, 1)

            sum_turns = ((0, 3), (1, 0), (1, 3), (2, 0))

            pe.wait_ge(onehot_in, 16)
            for j in range(G):
                sum_context(0, j)
            pe.wait_ge(const_in, 16 * N_CONST)
            transpose_context(0)
            pe.wait_ge(setup, 6)
            for c in range(KC):
                last = nc.tensor.matmul(out_ps[:, 0:ER + E], mean_w[:, :], aT_in[:, c, :], start=(c == 0),
                                        stop=(c == KC - 1))
            last.then_inc(mean_done, 1)
            next_norms(0)
            transpose_similarities(0)
            spread_similarities(0, 0, 0)
            spread_similarities(0, 0, 1)
            pe.wait_ge(weights_done, 5)

            def body(g, first, last):
                for j in range(G):
                    def before(k):
                        return (g, j - k) if j >= k else (g - 1, j - k + G)
                    one = j >= 1 or not first
                    two = j >= 2 or not first
                    for i in range(6):
                        if i < 4:
                            spread_similarities(g, j, i + 2)
                        elif j < 3:
                            spread_similarities(g, j + 1, i - 4)
                        elif not last:
                            spread_similarities(g + 1, 0, i - 4)
                        if i == 1 and one:
                            transpose_tokens(*before(1), 1)
                            experts_in(*before(1), 0)
                        if i == 2 and one:
                            experts_in(*before(1), 1)
                        if i == 3 and two:
                            transpose_hidden(*before(2), G * g + j - 1)
                        if i == 4 and two:
                            experts_out(*before(2), 0)
                        if i == 5 and two:
                            experts_out(*before(2), 1)
                        if i == 5:
                            transpose_tokens(g, j, 0)
                        if (j, i) in sum_turns and not last:
                            sum_context(g + 1, sum_turns.index((j, i)))
                        if i == 2 and j == 2 and not last:
                            transpose_context(g + 1)
                        if i == 5 and j == 2 and not last:
                            next_norms(g + 1)
                        if i == 2 and j == 3 and not last:
                            transpose_similarities(g + 1)
                        tap(g, j, i)

            each_group(pe, body)
            transpose_tokens(NG - 1, G - 1, 1)
            experts_in(NG - 1, G - 1, 0)
            experts_in(NG - 1, G - 1, 1)
            transpose_hidden(NG - 1, G - 2, B - 1)
            experts_out(NG - 1, G - 2, 0)
            experts_out(NG - 1, G - 2, 1)
            transpose_hidden(NG - 1, G - 1, B - 1)
            experts_out(NG - 1, G - 1, 0)
            experts_out(NG - 1, G - 1, 1)



def kernel(x, ctx_4096, g_xattn, g_ffn, L0_xattn_weight, L0_ffn_router_w, L0_ffn_router_b, L0_ffn_A, L0_ffn_Bm):
    import numpy as np
    import concourse.bacc as bacc
    from concourse.bass_utils import run_bass_kernel_spmd

    x, ctx = np.ascontiguousarray(x), np.ascontiguousarray(ctx_4096)
    weight, router_w = np.asarray(L0_xattn_weight), np.asarray(L0_ffn_router_w)
    a, bm = np.asarray(L0_ffn_A), np.asarray(L0_ffn_Bm)
    B, C, T = x.shape
    E, R, _ = a.shape

    conv_wT = np.ascontiguousarray(weight.transpose(1, 2, 0)).reshape(C, TAPS * P)
    rows_a = np.concatenate([a.reshape(E * R, T), router_w], axis=0)
    expert_aT = np.ascontiguousarray(rows_a.T.reshape(T // P, P, E * R + E).transpose(1, 0, 2))
    expert_b = np.ascontiguousarray(bm.transpose(0, 2, 1)).reshape(E * R, T)

    import ml_dtypes
    bf16 = ml_dtypes.bfloat16
    identity = np.eye(P, dtype=np.float32)
    one_hot = np.zeros((P, G, 32), np.float32)
    for b in range(G):
        one_hot[:, b, b] = 1.0
    shift = np.zeros((P, 2, P), np.float32)
    shift[np.arange(1, P), 0, np.arange(P - 1)] = 1.0
    shift[0, 1, P - 1] = 1.0
    select = np.zeros((96, G, TAPS, P), np.float32)
    for c in range(C):
        for k in range(TAPS):
            block = (2, 1, 0)[(c * TAPS + k) // C]
            for part in range(3):
                for b in range(G):
                    select[32 * block + G * part + b, b, k, c] = 1.0
    expert_ids = np.tile(np.arange(E, dtype=np.float32), (P, 1))

    arrays = dict(x=x, ctx=ctx, g_xattn=np.ascontiguousarray(g_xattn), g_ffn=np.ascontiguousarray(g_ffn),
                  conv_wT=conv_wT, expert_aT=expert_aT, router_b=np.ascontiguousarray(L0_ffn_router_b),
                  expert_b=expert_b, identity=identity, identity_bf=identity.astype(bf16), one_hot=one_hot,
                  shift=shift, select=select.astype(bf16), expert_ids=expert_ids)
    nc = bacc.Bacc("TRN2", target_bir_lowering=False, num_devices=1)
    ins = {n: nc.dram_tensor(n, v.shape, mybir.dt.from_np(v.dtype), kind="ExternalInput").ap()
           for n, v in arrays.items()}
    out = nc.dram_tensor("out", x.shape, F32, kind="ExternalOutput").ap()
    flamingo_kernel(nc, **ins, out=out)
    r = run_bass_kernel_spmd(nc, [arrays], core_ids=[0])
    return r.results[0]["out"]
```

```python
import concourse.bass as bass
from concourse import mybir
from contextlib import ExitStack

F32 = mybir.dt.float32
F32R = mybir.dt.float32r
BF16 = mybir.dt.bfloat16
I32 = mybir.dt.int32
U32 = mybir.dt.uint32
ALU = mybir.AluOpType
ACT = mybir.ActivationFunctionType

P = 128
HALF = 512
LN_EPS = 1e-5
COS_EPS = 1e-8
TAPS = 3
G = 4
WARM_UP = 7
WHOLE = ((), (4,), (4,), (3, 4))
LEAD = 2


def flamingo_kernel(nc, x, ctx, g_xattn, g_ffn, conv_wT, expert_aT, router_b, expert_b,
                    identity, identity_bf, one_hot, shift, select, expert_ids, out):
    B, C, T = x.shape
    NG = B // G
    KC = T // P
    E = router_b.shape[0]
    ER = expert_aT.shape[2] - E
    R = ER // E
    SCALING = 8.0 / R
    assert C == P and T == 2 * HALF and ER == P and B % G == 0 and NG >= 3

    st = ExitStack()
    with st:
        def sb(name, shape, dt=F32):
            return st.enter_context(nc.sbuf_tensor(name, shape, dt))

        def sem(name):
            return st.enter_context(nc.semaphore(name))

        ident = sb("ident", [P, P])
        identb = sb("identb", [P, P], BF16)
        onehot = sb("onehot", [P, G, 32])
        shifts = sb("shifts", [P, 2, P])
        sel = sb("sel", [96, G, TAPS, P], BF16)
        ids = sb("ids", [P, E])
        mean_w = sb("mean_w", [P, P])
        minus_half = sb("minus_half", [P, 1])
        eps = sb("eps", [P, 1])
        eps_t = sb("eps_t", [P, 1])
        minus_t = sb("minus_t", [P, 1])
        gates_in = sb("gates_in", [P, 2])
        gates_th = sb("gates_th", [P, 2])
        factors = sb("factors", [P, 2])
        gates = sb("gates", [P, 2])
        wT_in = sb("wT_in", [P, TAPS * P])
        wT = sb("wT", [P, TAPS * P])
        w_hi = sb("w_hi", [P, TAPS, P], F32R)
        w_lo = sb("w_lo", [P, TAPS, P], F32R)
        aT_in = sb("aT_in", [P, KC, ER + E])
        aT = sb("aT", [P, KC, ER + E])
        rb = sb("rb", [P, E])
        bm_in = sb("bm_in", [P, T])
        bm = sb("bm", [P, T])
        bm_hi = sb("bm_hi", [P, T], F32R)
        bm_lo = sb("bm_lo", [P, T], F32R)
        et = sb("et", [P, G, T])
        sq = sb("sq", [P, 2, T])
        pr = sb("pr", [P, 2, T])
        sums = sb("sums", [P, HALF])
        nd = sb("nd", [P, 4, G, G])
        nmax = sb("nmax", [P, KC, G])
        rinv = sb("rinv", [P, KC, G])
        guess = sb("guess", [P, KC * G])
        guess_n = sb("guess_n", [P, KC * G])
        excess = sb("excess", [P, KC * G])
        dr = sb("dr", [P, KC, G])
        nr = sb("nr", [P, KC, G])
        sim = sb("sim", [P, KC, 3, G])
        rest1 = sb("rest1", [P, KC, 3, G])
        rest2 = sb("rest2", [P, KC, 3, G])
        simp = sb("simp", [P, KC, 3, 32], BF16)
        rows = sb("rows", [96, NG, T], BF16)
        xt = sb("xt", [P, G, T])
        x1 = sb("x1", [P, G, T])
        unread = sb("unread", [P, 2, T])
        xsum = sb("xsum", [P, G])
        minus_mean = sb("minus_mean", [P, G])
        squares = sb("squares", [P, G])
        ve1 = sb("ve1", [P, G])
        rs1 = sb("rs1", [P, G])
        offset = sb("offset", [P, G])
        xn = sb("xn", [P, 2, T + 2])
        pt = sb("pt", [P, 6, HALF])
        pt_hi = sb("pt_hi", [P, 6, HALF], F32R)
        pt_lo = sb("pt_lo", [P, 6, HALF], F32R)
        bn2 = sb("bn2", [P, 2, 12])
        mv2 = sb("mv2", [P, 2, 2])
        ve2 = sb("ve2", [P, 2])
        rs2 = sb("rs2", [P, 2])
        xT = sb("xT", [P, 2, KC, P])
        logit = sb("logit", [P, E])
        top = sb("top", [P, 8])
        topi = sb("topi", [P, 8], U32)
        below = sb("below", [P, E])
        expo = sb("expo", [P, E])
        pick0 = sb("pick0", [P, E])
        pick = sb("pick", [P, E])
        expk = sb("expk", [P, E])
        esum = sb("esum", [P, 1])
        einv = sb("einv", [P, 1])
        gate = sb("gate", [P, E])
        hw = sb("hw", [P, 2, ER])
        hs = sb("hs", [P, 2, ER + E])
        hwT = sb("hwT", [P, 2, P])
        hwT_hi = sb("hwT_hi", [P, 2, P], F32R)
        hwT_lo = sb("hwT_lo", [P, 2, P], F32R)

        bank = [st.enter_context(nc.psum_tensor(f"bank{i}", [P, HALF], F32)) for i in range(8)]
        sim_ps = bank[0:2]
        conv_ps = bank[2:4]
        xT_ps = bank[4]
        out_ps = bank[5]
        h_ps = bank[6][:, 0:ER + E]
        hwT_ps = bank[6][:, 256:256 + P]
        last_hwT_ps = [bank[0][:, 0:P], bank[0][:, P:2 * P]]
        last_out_ps = [bank[2], bank[1], bank[3], bank[4]]
        sum_ps = bank[7]
        ctxT_ps = bank[7][:, :].rearrange("p (w q b) -> p q w b", w=4, q=4)
        rnext_ps = bank[7][:, 0:KC * G]
        rows_ps = bank[7][:, :].bitcast(BF16)

        onehot_in = sem("onehot_in")
        ident_in = sem("ident_in")
        conv_in = sem("conv_in")
        attn_in = sem("attn_in")
        aT_in_done = sem("aT_in_done")
        ffn_in = sem("ffn_in")
        bm_in_done = sem("bm_in_done")
        e_in = [sem(f"e_in{j}") for j in range(G)]
        x_in = [sem(f"x_in{j}") for j in range(G)]
        stored = [sem(f"stored{j}") for j in range(G)]
        setup = sem("setup")
        tanh_done = sem("tanh_done")
        mean_done = sem("mean_done")
        wT_done = sem("wT_done")
        w_hi_done = sem("w_hi_done")
        w_lo_done = sem("w_lo_done")
        gates_done = sem("gates_done")
        aT_done = sem("aT_done")
        bm_done = sem("bm_done")
        bm_hi_done = sem("bm_hi_done")
        bm_lo_done = sem("bm_lo_done")
        newton = sem("newton")
        sq_done = sem("sq_done")
        pr_done = [sem("pr_even_done"), sem("pr_odd_done")]
        summed = sem("summed")
        sums_out = sem("sums_out")
        ctxT_done = sem("ctxT_done")
        nd_done = sem("nd_done")
        nmax_done = sem("nmax_done")
        rinv_done = sem("rinv_done")
        rnext_done = sem("rnext_done")
        partial = sem("partial")
        sim_done = sem("sim_done")
        split = sem("split")
        rowsT_done = sem("rowsT_done")
        rows_done = sem("rows_done")
        xsum_done = sem("xsum_done")
        minus_mean_done = sem("minus_mean_done")
        squares_done = sem("squares_done")
        ve1_done = sem("ve1_done")
        rs1_done = sem("rs1_done")
        offset_done = sem("offset_done")
        xn_done = sem("xn_done")
        spread = sem("spread")
        mod_done = sem("mod_done")
        hi_done = sem("hi_done")
        lo_done = sem("lo_done")
        tap_done = sem("tap_done")
        x1_done = sem("x1_done")
        bn2_done = sem("bn2_done")
        mv2_done = sem("mv2_done")
        ve2_done = sem("ve2_done")
        rs2_done = sem("rs2_done")
        xT_done = sem("xT_done")
        xT_out = sem("xT_out")
        h_done = sem("h_done")
        h_out = sem("h_out")
        logit_done = sem("logit_done")
        top_done = sem("top_done")
        topi_done = sem("topi_done")
        below_done = sem("below_done")
        expo_done = sem("expo_done")
        pick0_done = sem("pick0_done")
        pick_done = sem("pick_done")
        esum_done = sem("esum_done")
        einv_done = sem("einv_done")
        gate_done = sem("gate_done")
        hw_done = sem("hw_done")
        hwT_done = sem("hwT_done")
        hwT_out = sem("hwT_out")
        hwT_rest = sem("hwT_rest")
        ffn_done = sem("ffn_done")
        out_done = sem("out_done")

        block = st.enter_context(nc.Block())

        def each_group(eng, body):
            body(0, True, False)
            with eng.Fori(1, NG - 1) as g:
                body(g, False, False)
            body(NG - 1, False, True)

        def shifted(g, j, i, k):
            b = j + (i + k) // 6
            return (g, b, (i + k) % 6) if b < G else (g + 1, b - G, (i + k) % 6)

        def first_batch(g, j):
            return isinstance(g, int) and G * g + j == 0

        def whole(g, j, i):
            return i in WHOLE[j] or first_batch(g, j)

        def parts_before(g, j, i):
            count = [6 - len(steps) for steps in WHOLE]
            return sum(count) * g + sum(count[:j]) - count[0] + sum(m not in WHOLE[j] for m in range(i))

        def past(g, j, k):
            return not isinstance(g, int) or G * g + j >= k

        def half(h):
            return slice(h * HALF, (h + 1) * HALF)

        @block.sync
        def _(sp):
            def load_e(g, j):
                if past(g, 0, 1):
                    sp.wait_ge(sq_done, G * g + j - G + 1)
                    sp.wait_ge(pr_done[j % 2], 2 * (g - 1) + j // 2 + 1)
                sp.dma_start(et[:, j, :], ctx[G * g + j, :, :]).then_inc(e_in[j], 16)

            def load_x(g, j):
                if past(g, 0, 1):
                    sp.wait_ge(x1_done, 2 * (G * g + j - G + 1))
                sp.dma_start(xt[:, j, :], x[G * g + j, :, :]).then_inc(x_in[j], 16)

            def store(g, j):
                sp.wait_ge(out_done, 2 * (G * g + j + 1))
                sp.dma_start(out[G * g + j, :, :], x1[:, j, :]).then_inc(stored[j], 16)

            load_e(0, 0)
            sp.dma_start(onehot[:, :, :], one_hot).then_inc(onehot_in, 16)
            load_e(0, 1)
            load_e(0, 2)
            load_e(0, 3)
            sp.dma_start(ident[:, :], identity).then_inc(ident_in, 16)
            load_x(0, 0)
            sp.dma_start(aT_in[:, :, :], expert_aT).then_inc(aT_in_done, 16)
            sp.dma_start(gates_in[:, 0:1], g_xattn.rearrange("(a n) -> a n", a=1).to_broadcast([P, 1])).then_inc(conv_in, 16)
            sp.dma_start(gates_in[:, 1:2], g_ffn.rearrange("(a n) -> a n", a=1).to_broadcast([P, 1])).then_inc(conv_in, 16)
            sp.dma_start(wT_in[:, :], conv_wT).then_inc(conv_in, 16)
            sp.dma_start(shifts[:, :, :], shift).then_inc(attn_in, 16)
            sp.dma_start(identb[:, :], identity_bf).then_inc(attn_in, 16)
            sp.dma_start(sel[:, :, :, :], select).then_inc(attn_in, 16)
            load_x(0, 1)
            sp.dma_start(ids[:, :], expert_ids).then_inc(ffn_in, 16)
            sp.dma_start(rb[:, :], router_b.rearrange("(a n) -> a n", a=1).to_broadcast([P, E])).then_inc(ffn_in, 16)
            load_x(0, 2)
            sp.dma_start(bm_in[:, :], expert_b).then_inc(bm_in_done, 16)
            for j in range(G):
                load_e(1, j)
            load_x(0, 3)

            def body(g, first, last):
                for j in range(G):
                    if j > 0 and not last:
                        load_x(g + 1, j - 1)
                    if j == 0 and not first:
                        load_x(g, G - 1)
                    if j == 1 and not last and not (isinstance(g, int) and g + 2 >= NG):
                        load_e(g + 2, 0)
                        load_e(g + 2, 1)
                    if j == 2 and not last and not (isinstance(g, int) and g + 2 >= NG):
                        load_e(g + 2, 2)
                        load_e(g + 2, 3)
                    if j >= 3:
                        store(g, j - 3)
                    elif not first:
                        store(g - 1, j + 1)

            body(0, True, False)
            with sp.Fori(1, NG - 2) as g:
                body(g, False, False)
            body(NG - 2, False, False)
            body(NG - 1, False, True)
            for j in range(1, G - 1):
                store(NG - 1, j)
            for h in range(2):
                sp.wait_ge(out_done, 2 * B - 1 + h)
                sp.dma_start(out[B - 1, :, half(h)], x1[:, G - 1, half(h)]).then_inc(stored[G - 1], 16)
            for j in range(G):
                sp.wait_ge(stored[j], 16 * (NG + j // (G - 1)))

        @block.gpsimd
        def _(pool):
            nc.gpsimd.memset(eps[:, :], LN_EPS).then_inc(setup, 1)
            nc.gpsimd.memset(eps_t[:, :], LN_EPS * T).then_inc(setup, 1)
            nc.gpsimd.memset(minus_t[:, :], -1.0 / T).then_inc(setup, 1)
            nc.gpsimd.memset(factors[:, 0:1], T ** 0.5).then_inc(setup, 1)
            nc.gpsimd.memset(factors[:, 1:2], SCALING).then_inc(setup, 1)
            nc.gpsimd.memset(minus_half[:, :], -0.5).then_inc(setup, 1)
            nc.gpsimd.memset(mean_w[:, :], 1.0 / T).then_inc(setup, 1)
            nc.gpsimd.memset(pr[:, :, T - 1:T], 0.0).then_inc(setup, 1)
            nc.gpsimd.memset(simp[:, :, :, :], 0.0).then_inc(setup, 1)
            nc.gpsimd.memset(xn[:, :, 0:T + 2:T + 1], 0.0).then_inc(setup, 1)
            pool.wait_ge(setup, 11)

            def product(g, j):
                if past(g, j, 2):
                    pool.wait_ge(summed, G * g + j - 1)
                pool.wait_ge(e_in[j], 16 * (g + 1))
                nc.gpsimd.tensor_tensor(pr[:, j % 2, 0:T - 1], et[:, j, 0:T - 1], et[:, j, 1:T],
                                        ALU.mult).then_inc(pr_done[1], 1)

            def feature_mean(g, j):
                pool.wait_ge(xsum_done, G * g + j + 1)
                nc.gpsimd.tensor_tensor(minus_mean[:, j:j + 1], xsum[:, j:j + 1], minus_t[:, :],
                                        ALU.mult).then_inc(minus_mean_done, 1)

            def feature_rstd(g, j):
                pool.wait_ge(squares_done, G * g + j + 1)
                nc.gpsimd.tensor_tensor(ve1[:, j:j + 1], squares[:, j:j + 1], eps_t[:, :], ALU.add).then_inc(ve1_done, 1)
                pool.wait_ge(ve1_done, G * g + j + 1)
                nc.gpsimd.tensor_tensor(rs1[:, j:j + 1], ve1[:, j:j + 1], minus_half[:, 0:1],
                                        ALU.pow).then_inc(rs1_done, 1)
                pool.wait_ge(rs1_done, G * g + j + 1)
                nc.gpsimd.tensor_tensor(offset[:, j:j + 1], minus_mean[:, j:j + 1], rs1[:, j:j + 1],
                                        ALU.mult).then_inc(offset_done, 1)

            def modulated_rest(g, j, i):
                n = 6 * (G * g + j) + i
                pool.wait_ge(hi_done, parts_before(g, j, i) + 1)
                if not (isinstance(g, int) and n < 6):
                    pool.wait_ge(tap_done, n - 5)
                nc.gpsimd.tensor_tensor(pt_lo[:, i, :], pt[:, i, :], pt_hi[:, i, :],
                                        ALU.subtract).then_inc(lo_done, 1)

            def hidden(g, j):
                i, n = j % 2, G * g + j
                pool.wait_ge(gate_done, n + 1)
                if past(g, j, 2):
                    pool.wait_ge(hwT_done, n - 1)
                nc.gpsimd.tensor_tensor(hw[:, i, :].rearrange("p (e r) -> p e r", e=E),
                                        hs[:, i, 0:ER].rearrange("p (e r) -> p e r", e=E),
                                        gate[:, :].unsqueeze(2).to_broadcast([P, E, R]),
                                        ALU.mult).then_inc(hw_done, 1)

            def hidden_rest(g, j):
                i, n = j % 2, G * g + j
                pool.wait_ge(hwT_out, 2 * (n + 1))
                if past(g, j, 2):
                    pool.wait_ge(ffn_done, 2 * (n - 1))
                nc.gpsimd.tensor_tensor(hwT_lo[:, i, :], hwT[:, i, :], hwT_hi[:, i, :],
                                        ALU.subtract).then_inc(hwT_rest, 1)

            def token_rstd(g, j):
                i = j % 2
                pool.wait_ge(mv2_done, G * g + j + 1)
                nc.gpsimd.tensor_tensor(ve2[:, i:i + 1], mv2[:, i, 1:2], eps[:, :], ALU.add).then_inc(ve2_done, 1)
                pool.wait_ge(ve2_done, G * g + j + 1)
                nc.gpsimd.tensor_tensor(rs2[:, i:i + 1], ve2[:, i:i + 1], minus_half[:, 0:1],
                                        ALU.pow).then_inc(rs2_done, 1)

            feature_mean(0, 0)
            feature_rstd(0, 0)
            pool.wait_ge(tanh_done, 1)
            nc.gpsimd.tensor_tensor(gates[:, :], gates_th[:, :], factors[:, :], ALU.mult).then_inc(gates_done, 1)
            pool.wait_ge(w_hi_done, 1)
            nc.gpsimd.tensor_tensor(w_lo[:, :, :].rearrange("p k o -> p (k o)"), wT[:, :],
                                    w_hi[:, :, :].rearrange("p k o -> p (k o)"), ALU.subtract).then_inc(w_lo_done, 1)
            feature_mean(0, 1)
            feature_rstd(0, 1)

            def body(g, first, last):
                for j in range(G):
                    def before(k):
                        return (g, j - k) if j >= k else (g - 1, j - k + G)
                    one = j >= 1 or not first
                    two = j >= 2 or not first
                    ahead = (g, j + 2) if j < 2 else (g + 1, j - 2)
                    stats = j < 2 or not last
                    def rest(i):
                        step = shifted(g, j, i, LEAD)
                        if not whole(*step) and not (last and j + (i + LEAD) // 6 == G):
                            modulated_rest(*step)

                    rest(0)
                    if j == 1 and not last:
                        product(g + 1, 3)
                    rest(1)
                    if two:
                        hidden(*before(2))
                    if j == 0 and not last:
                        product(g + 1, 1)
                    rest(2)
                    if one:
                        token_rstd(*before(1))
                    rest(3)
                    if stats:
                        feature_mean(*ahead)
                    if j == 0 and first:
                        pool.wait_ge(bm_hi_done, 1)
                        nc.gpsimd.tensor_tensor(bm_lo[:, :], bm[:, :], bm_hi[:, :],
                                                ALU.subtract).then_inc(bm_lo_done, 1)
                    if two:
                        hidden_rest(*before(2))
                    rest(4)
                    if stats:
                        feature_rstd(*ahead)
                    rest(5)

            each_group(pool, body)
            token_rstd(NG - 1, G - 1)
            hidden(NG - 1, G - 2)
            hidden_rest(NG - 1, G - 2)
            hidden(NG - 1, G - 1)
            hidden_rest(NG - 1, G - 1)

        @block.scalar
        def _(act):
            def square(g, j):
                if past(g, j, 2):
                    act.wait_ge(summed, G * g + j - 1)
                act.wait_ge(e_in[j], 16 * (g + 1))
                nc.scalar.activation(sq[:, j % 2, :], et[:, j, :], ACT.Square).then_inc(sq_done, 1)

            def sums_evacuate(g):
                act.wait_ge(summed, G * (g + 1))
                if past(g, 0, 1):
                    act.wait_ge(ctxT_done, g)
                nc.scalar.activation(sums[:, :], sum_ps[:, :], ACT.Copy).then_inc(sums_out, 1)

            def rows_left(g):
                act.wait_ge(rowsT_done, g + 1)
                nc.scalar.activation(rows[64:96, g, 1:T], rows_ps[64:96, 0:T - 1], ACT.Copy).then_inc(rows_done, 1)

            def rows_evacuate(g):
                rows_left(g)
                nc.scalar.activation(rows[0:64, g, :], rows_ps[0:64, :], ACT.Copy).then_inc(rows_done, 1)

            def feature_sum(g, j):
                n = G * g + j
                act.wait_ge(x_in[j], 16 * (g + 1))
                if past(g, j, 1):
                    act.wait_ge(squares_done, n)
                nc.scalar.activation(unread[:, 0, :], xt[:, j, :], ACT.Copy,
                                     accum_out=xsum[:, j:j + 1]).then_inc(xsum_done, 1)

            def feature_squares(g, j):
                act.wait_ge(minus_mean_done, G * g + j + 1)
                nc.scalar.activation(unread[:, 1, :], xt[:, j, :], ACT.Square, bias=minus_mean[:, j:j + 1],
                                     accum_out=squares[:, j:j + 1]).then_inc(squares_done, 1)

            def normalize(g, j):
                n = G * g + j
                act.wait_ge(offset_done, n + 1)
                if past(g, j, 2):
                    act.wait_ge(mod_done, 6 * (n - 1))
                nc.scalar.activation(xn[:, j % 2, 1:T + 1], xt[:, j, :], ACT.Identity, bias=offset[:, j:j + 1],
                                     scale=rs1[:, j:j + 1]).then_inc(xn_done, 1)

            def modulated_hi(g, j, i):
                n = 6 * (G * g + j) + i
                act.wait_ge(mod_done, n + 1)
                if not (isinstance(g, int) and n < 6):
                    act.wait_ge(tap_done, n - 5)
                nc.scalar.activation(pt_hi[:, i, :], pt[:, i, :], ACT.Copy).then_inc(hi_done, 1)

            def tokens_evacuate(g, j, h):
                act.wait_ge(xT_done, 2 * (G * g + j) + h + 1)
                if past(g, j, 2):
                    act.wait_ge(h_done, G * g + j - 1)
                nc.scalar.activation(xT[:, j % 2, 4 * h:4 * h + 4, :].rearrange("p c n -> p (c n)"),
                                     xT_ps[:, :], ACT.Copy).then_inc(xT_out, 1)

            def exponent(g, j):
                act.wait_ge(below_done, G * g + j + 1)
                if past(g, j, 1):
                    act.wait_ge(esum_done, G * g + j)
                nc.scalar.activation(expo[:, :], below[:, :], ACT.Exp).then_inc(expo_done, 1)

            def logits_evacuate(g, j):
                n = G * g + j
                act.wait_ge(h_done, n + 1)
                if past(g, j, 2):
                    act.wait_ge(hw_done, n - 1)
                nc.scalar.activation(hs[:, j % 2, :], h_ps, ACT.Copy).then_inc(h_out, 1)

            def hidden_evacuate(g, j, source=hwT_ps):
                i, n = j % 2, G * g + j
                act.wait_ge(hwT_done, n + 1)
                if past(g, j, 2):
                    act.wait_ge(ffn_done, 2 * (n - 1))
                nc.scalar.activation(hwT[:, i, :], source, ACT.Copy).then_inc(hwT_out, 1)
                nc.scalar.activation(hwT_hi[:, i, :], source, ACT.Copy).then_inc(hwT_out, 1)

            square(0, 0)
            square(0, 1)
            square(0, 2)
            square(0, 3)
            feature_sum(0, 0)
            sums_evacuate(0)
            feature_squares(0, 0)
            act.wait_ge(conv_in, 16 * 3)
            nc.scalar.activation(gates_th[:, :], gates_in[:, :], ACT.Tanh).then_inc(tanh_done, 1)
            normalize(0, 0)
            act.wait_ge(gates_done, 1)
            nc.scalar.activation(wT[:, :], wT_in[:, :], ACT.Copy, scale=gates[:, 0:1]).then_inc(wT_done, 1)
            act.wait_ge(wT_done, 1)
            nc.scalar.activation(w_hi[:, :, :].rearrange("p k o -> p (k o)"), wT[:, :], ACT.Copy).then_inc(w_hi_done, 1)
            feature_sum(0, 1)
            feature_squares(0, 1)
            act.wait_ge(setup, 11)
            rows_left(0)

            def body(g, first, last):
                for j in range(G):
                    def before(k):
                        return (g, j - k) if j >= k else (g - 1, j - k + G)
                    one = j >= 1 or not first
                    two = j >= 2 or not first
                    ahead = (g, j + 2) if j < 2 else (g + 1, j - 2)
                    stats = j < 2 or not last
                    def high(i):
                        step = shifted(g, j, i, LEAD)
                        if not whole(*step) and not (last and j + (i + LEAD) // 6 == G):
                            modulated_hi(*step)

                    high(0)
                    if j == 0 and not last:
                        square(g + 1, 0)
                    if j == 3 and not last:
                        rows_evacuate(g + 1)
                    high(1)
                    if j < 3:
                        normalize(g, j + 1)
                    elif not last:
                        normalize(g + 1, 0)
                    if j == 1 and not last:
                        square(g + 1, 3)
                    if one:
                        tokens_evacuate(*before(1), 1)
                    high(2)
                    if stats:
                        feature_sum(*ahead)
                    if j == 0 and not last:
                        square(g + 1, 1)
                    if j == 0 and first:
                        act.wait_ge(bm_in_done, 16)
                        nc.scalar.activation(bm[:, :], bm_in[:, :], ACT.Copy, scale=gates[:, 1:2]).then_inc(bm_done, 1)
                        act.wait_ge(bm_done, 1)
                        nc.scalar.activation(bm_hi[:, :], bm[:, :], ACT.Copy).then_inc(bm_hi_done, 1)
                    high(3)
                    if one:
                        logits_evacuate(*before(1))
                    high(4)
                    if two:
                        hidden_evacuate(*before(2))
                    if stats:
                        feature_squares(*ahead)
                    if j == 1 and not last:
                        sums_evacuate(g + 1)
                    high(5)
                    if j == 0 and not last:
                        square(g + 1, 2)
                    if one:
                        exponent(*before(1))
                    tokens_evacuate(g, j, 0)

            each_group(act, body)
            tokens_evacuate(NG - 1, G - 1, 1)
            logits_evacuate(NG - 1, G - 1)
            hidden_evacuate(NG - 1, G - 2, last_hwT_ps[0])
            exponent(NG - 1, G - 1)
            hidden_evacuate(NG - 1, G - 1, last_hwT_ps[1])

        @block.vector
        def _(dve):
            def context_columns(g):
                dve.wait_ge(ctxT_done, g + 1)
                nc.vector.tensor_copy(nd[:, :, :, :], ctxT_ps[:, :, :, 0:G]).then_inc(nd_done, 1)
                dve.wait_ge(nd_done, g + 1)
                nc.vector.tensor_scalar(nmax[:, :, :].rearrange("p a b -> p (a b)"),
                                        nd[:, 0:2, :, :].rearrange("p h w b -> p (h w b)"),
                                        COS_EPS * COS_EPS, None, ALU.max).then_inc(nmax_done, 1)

            def inverse_norms(g):
                n_all = nmax[:, :, :].rearrange("p a b -> p (a b)")
                result = rinv[:, :, :].rearrange("p a b -> p (a b)")
                dve.wait_ge(nmax_done, g + 1)
                nc.vector.tensor_scalar(guess[:, :].bitcast(I32), n_all.bitcast(I32), -0.5, float(0x5f3759df),
                                        ALU.mult, ALU.add).then_inc(newton, 1)
                yield
                for step in range(3):
                    dve.wait_ge(newton, 9 * g + 3 * step + 1)
                    nc.vector.scalar_tensor_tensor(out=guess_n[:, :], in0=guess[:, :], scalar=-0.5, in1=n_all,
                                                   op0=ALU.mult, op1=ALU.mult).then_inc(newton, 1)
                    yield
                    dve.wait_ge(newton, 9 * g + 3 * step + 2)
                    nc.vector.tensor_tensor(excess[:, :], guess_n[:, :], guess[:, :], ALU.mult).then_inc(newton, 1)
                    yield
                    dve.wait_ge(newton, 9 * g + 3 * step + 3)
                    nc.vector.scalar_tensor_tensor(out=result if step == 2 else guess[:, :], in0=excess[:, :],
                                                   scalar=1.5, in1=guess[:, :], op0=ALU.add,
                                                   op1=ALU.mult).then_inc(rinv_done if step == 2 else newton, 1)
                    yield

            norms = nd[:, 0:2, :, :].rearrange("p h w b -> p (h w) b")
            dots = nd[:, 2:4, :, :].rearrange("p h w b -> p (h w) b")

            def similarities(g):
                dve.wait_ge(rinv_done, g + 1)
                nc.vector.tensor_tensor(dr[:, :, :], dots, rinv[:, :, :], ALU.mult).then_inc(partial, 1)
                nc.vector.tensor_tensor(nr[:, :, :], norms, rinv[:, :, :], ALU.mult).then_inc(partial, 1)
                dve.wait_ge(rnext_done, g + 1)
                dve.wait_ge(partial, 2 * (g + 1))
                nc.vector.tensor_tensor(sim[:, :, 0:3:2, :],
                                        dr[:, :, :].unsqueeze(2).to_broadcast([P, KC, 2, G]),
                                        rnext_ps.rearrange("p (a b) -> p a b", b=G).unsqueeze(2).to_broadcast([P, KC, 2, G]),
                                        ALU.mult).then_inc(sim_done, 1)
                nc.vector.tensor_tensor(sim[:, :, 1, :], nr[:, :, :], rinv[:, :, :], ALU.mult).then_inc(sim_done, 1)

            def split_similarities(g):
                part = [simp[:, :, :, G * i:G * i + G] for i in range(3)]
                dve.wait_ge(sim_done, 2 * (g + 1))
                nc.vector.tensor_copy(part[0], sim[:, :, :, :]).then_inc(split, 1)
                yield
                dve.wait_ge(split, 5 * g + 1)
                nc.vector.tensor_tensor(rest1[:, :, :, :], sim[:, :, :, :], part[0], ALU.subtract).then_inc(split, 1)
                yield
                dve.wait_ge(split, 5 * g + 2)
                nc.vector.tensor_copy(part[1], rest1[:, :, :, :]).then_inc(split, 1)
                yield
                dve.wait_ge(split, 5 * g + 3)
                nc.vector.tensor_tensor(rest2[:, :, :, :], rest1[:, :, :, :], part[1], ALU.subtract).then_inc(split, 1)
                yield
                dve.wait_ge(split, 5 * g + 4)
                nc.vector.tensor_copy(part[2], rest2[:, :, :, :]).then_inc(split, 1)
                yield

            def modulate(g, j, i):
                n = 6 * (G * g + j) + i
                h, k = i // TAPS, i % TAPS
                if i == 0:
                    dve.wait_ge(xn_done, G * g + j + 1)
                dve.wait_ge(spread, n + 1)
                if past(g, j, 1):
                    last = (g, j - 1, i) if j > 0 else (g - 1, G - 1, i)
                    if whole(*last):
                        dve.wait_ge(tap_done, n - 5)
                    else:
                        dve.wait_ge(lo_done, parts_before(*last) + 1)
                nc.vector.tensor_tensor(pt[:, i, :], xn[:, j % 2, h * HALF + k:(h + 1) * HALF + k],
                                        sim_ps[i % 2][:, :], ALU.mult).then_inc(mod_done, 1)

            def next_product(g, j):
                if past(g, j, 2):
                    dve.wait_ge(summed, G * g + j - 1)
                dve.wait_ge(e_in[j], 16 * (g + 1))
                nc.vector.tensor_tensor(pr[:, j % 2, 0:T - 1], et[:, j, 0:T - 1], et[:, j, 1:T],
                                        ALU.mult).then_inc(pr_done[j % 2], 1)

            def residual(g, j, h):
                n = G * g + j
                dve.wait_ge(tap_done, 6 * n + 3 * (h + 1))
                if h == 0 and not (isinstance(g, int) and g == 0):
                    dve.wait_ge(stored[j], 16 * g)
                nc.vector.tensor_tensor(x1[:, j, half(h)], conv_ps[h][:, :], xt[:, j, half(h)],
                                        ALU.add).then_inc(x1_done, 1)

            def token_stats(g, j, h):
                n = G * g + j
                dve.wait_ge(x1_done, 2 * n + h + 1)
                nc.vector.bn_stats(bn2[:, j % 2, 6 * h:6 * h + 6], x1[:, j, half(h)]).then_inc(bn2_done, 1)

            def token_stats_in(g, j):
                dve.wait_ge(bn2_done, 2 * (G * g + j + 1))

            def logits_in(g, j):
                dve.wait_ge(logit_done, G * g + j + 1)

            def token_variance(g, j):
                nc.vector.bn_aggr(mv2[:, j % 2, :], bn2[:, j % 2, :]).then_inc(mv2_done, 1)

            def pick_experts(g, j):
                n = G * g + j
                if isinstance(g, int) and n == 0:
                    dve.wait_ge(ffn_in, 16 * 2)
                dve.wait_ge(rs2_done, n + 1)
                dve.wait_ge(h_out, n + 1)
                nc.vector.scalar_tensor_tensor(out=logit[:, :], in0=hs[:, j % 2, ER:ER + E],
                                               scalar=rs2[:, j % 2:j % 2 + 1], in1=rb[:, :],
                                               op0=ALU.mult, op1=ALU.add).then_inc(logit_done, 1)
                yield
                nc.vector.max(top[:, :], logit[:, :]).then_inc(top_done, 1)
                yield
                dve.wait_ge(top_done, n + 1)
                nc.vector.tensor_scalar(below[:, :], logit[:, :], top[:, 0:1], None, ALU.subtract).then_inc(below_done, 1)
                nc.vector.max_index(topi[:, :], top[:, :], logit[:, :]).then_inc(topi_done, 1)
                yield

            def weigh_experts(g, j):
                n = G * g + j
                dve.wait_ge(topi_done, n + 1)
                nc.vector.tensor_scalar(pick0[:, :], ids[:, :], topi[:, 0:1], None, ALU.is_equal).then_inc(pick0_done, 1)
                yield
                dve.wait_ge(pick0_done, n + 1)
                nc.vector.scalar_tensor_tensor(out=pick[:, :], in0=ids[:, :], scalar=topi[:, 1:2], in1=pick0[:, :],
                                               op0=ALU.is_equal, op1=ALU.add).then_inc(pick_done, 1)
                yield

                dve.wait_ge(pick_done, n + 1)
                dve.wait_ge(expo_done, n + 1)
                nc.vector.scalar_tensor_tensor(out=expk[:, :], in0=expo[:, :], scalar=1.0, in1=pick[:, :],
                                               op0=ALU.mult, op1=ALU.mult, accum_out=esum[:, :]).then_inc(esum_done, 1)
                yield
                dve.wait_ge(esum_done, n + 1)
                nc.vector.reciprocal(einv[:, :], esum[:, :]).then_inc(einv_done, 1)
                yield
                dve.wait_ge(einv_done, n + 1)
                if past(g, j, 1):
                    dve.wait_ge(hw_done, n)
                nc.vector.tensor_scalar(gate[:, :], expk[:, :], einv[:, :], rs2[:, j % 2:j % 2 + 1], ALU.mult,
                                        ALU.mult).then_inc(gate_done, 1)
                yield

            def finish(g, j, h, source=out_ps):
                n = G * g + j
                dve.wait_ge(ffn_done, 2 * n + h + 1)
                nc.vector.tensor_tensor(x1[:, j, half(h)], source[:, :], x1[:, j, half(h)],
                                        ALU.add).then_inc(out_done, 1)

            nc.vector.memset(rows[64:96, :, 0:1], 0.0).then_inc(setup, 1)
            dve.wait_ge(setup, 11)
            for j in range(G):
                next_product(0, j)
            context_columns(0)
            for _ in inverse_norms(0):
                pass
            similarities(0)
            for _ in split_similarities(0):
                pass
            dve.wait_ge(rowsT_done, 1)
            nc.vector.tensor_copy(rows[0:64, 0, :], rows_ps[0:64, :]).then_inc(rows_done, 1)

            for i in range(LEAD):
                modulate(0, 0, i)

            def body(g, first, last):
                roots = parts = iter(())
                for j in range(G):
                    def before(k):
                        return (g, j - k) if j >= k else (g - 1, j - k + G)
                    one = j >= 1 or not first
                    two = j >= 2 or not first
                    three = j >= 3 or not first
                    nothing = iter(())
                    picks = pick_experts(*before(1)) if one else nothing
                    weights = weigh_experts(*before(2)) if two else nothing

                    def steps(of, n=1):
                        for _ in range(n):
                            next(of, None)

                    def ahead(i):
                        if not (last and j + (i + LEAD) // 6 == G):
                            modulate(*shifted(g, j, i, LEAD))

                    ahead(0)
                    if j == 0 and not last:
                        next_product(g + 1, 0)
                    steps(parts)
                    steps(weights)
                    steps(parts)
                    steps(parts)
                    steps(weights)
                    steps(parts)
                    ahead(1)
                    if j == 2 and not last:
                        context_columns(g + 1)
                        roots = inverse_norms(g + 1)
                    steps(weights)
                    steps(parts)
                    if one:
                        residual(*before(1), 1)
                    steps(weights)
                    steps(roots)
                    if three:
                        finish(*before(3), 0)
                    steps(weights)
                    steps(roots)
                    ahead(2)
                    steps(roots, 2)
                    if one:
                        token_stats(*before(1), 1)
                        steps(roots)
                        token_stats_in(*before(1))
                    ahead(3)
                    steps(roots)
                    if one:
                        token_variance(*before(1))
                    if three:
                        finish(*before(3), 1)
                    steps(roots)
                    ahead(4)
                    if j == 0 and not last:
                        next_product(g + 1, 2)
                    steps(roots)
                    if j == 0 and first:
                        dve.wait_ge(mean_done, 1)
                        nc.vector.tensor_tensor(aT[:, :, :], aT_in[:, :, :],
                                                out_ps[:, 0:ER + E].unsqueeze(1).to_broadcast([P, KC, ER + E]),
                                                ALU.subtract).then_inc(aT_done, 1)
                    steps(picks)
                    steps(roots)
                    if one:
                        logits_in(*before(1))
                    residual(g, j, 0)
                    steps(roots)
                    steps(picks)
                    steps(roots)
                    ahead(5)
                    steps(roots)
                    steps(picks)
                    steps(roots)
                    token_stats(g, j, 0)
                    if j == 2 and not last:
                        similarities(g + 1)
                        parts = split_similarities(g + 1)
                        steps(parts)

            each_group(dve, body)
            weights = weigh_experts(NG - 1, G - 2)
            residual(NG - 1, G - 1, 1)
            next(weights)
            next(weights)
            token_stats(NG - 1, G - 1, 1)
            next(weights)
            token_stats_in(NG - 1, G - 1)
            token_variance(NG - 1, G - 1)
            next(weights)
            finish(NG - 1, G - 3, 0)
            next(weights)
            picks = pick_experts(NG - 1, G - 1)
            next(picks)
            logits_in(NG - 1, G - 1)
            for _ in picks:
                pass
            weights = weigh_experts(NG - 1, G - 1)
            for _ in range(5):
                next(weights)
            finish(NG - 1, G - 3, 1)
            for h in range(2):
                finish(NG - 1, G - 2, h, last_out_ps[h])
            for h in range(2):
                finish(NG - 1, G - 1, h, last_out_ps[2 + h])

        @block.tensor
        def _(pe):
            def sum_context(g, j):
                pe.wait_ge(sq_done, G * g + j + 1)
                pe.wait_ge(pr_done[j % 2], 2 * g + j // 2 + 1)
                if j == 0 and not (isinstance(g, int) and g == 0):
                    pe.wait_ge(rows_done, 2 * g)
                for q, src in enumerate((sq, sq, pr, pr)):
                    last = nc.tensor.matmul(sum_ps[32 * q:32 * q + 32, :], onehot[:, j, :],
                                            src[:, j % 2, half(q % 2)], start=(j == 0), stop=(j == G - 1))
                last.then_inc(summed, 1)

            def transpose_context(g):
                pe.wait_ge(sums_out, g + 1)
                for w in range(4):
                    last = nc.tensor.transpose(sum_ps[:, w * P:(w + 1) * P], sums[:, w * P:(w + 1) * P], ident[:, :])
                last.then_inc(ctxT_done, 1)

            def next_norms(g):
                pe.wait_ge(rinv_done, g + 1)
                r = rinv[:, :, :].rearrange("p a b -> p (a b)")
                nc.tensor.matmul(rnext_ps, shifts[:, 0, :], r, start=True, stop=False)
                nc.tensor.matmul(rnext_ps[:, 0:(KC - 1) * G], shifts[:, 1, :], r[:, G:KC * G],
                                 start=False, stop=True).then_inc(rnext_done, 1)

            def transpose_similarities(g):
                pe.wait_ge(split, 5 * (g + 1))
                for c in range(KC):
                    last = nc.tensor.transpose(rows_ps[0:96, c * P:(c + 1) * P],
                                               simp[:, c, :, :].rearrange("p f q -> p (f q)"), identb[:, :])
                last.then_inc(rowsT_done, 1)

            def spread_similarities(g, j, i):
                n = 6 * (G * g + j) + i
                h, k = i // TAPS, i % TAPS
                if i == 0:
                    pe.wait_ge(rows_done, 2 * (g + 1))
                if not (isinstance(g, int) and n < 2):
                    pe.wait_ge(mod_done, n - 1)
                nc.tensor.matmul(sim_ps[i % 2][:, :], sel[:, j, k, :], rows[:, g, half(h)],
                                 start=True, stop=True).then_inc(spread, 1)

            def tap(g, j, i):
                n = 6 * (G * g + j) + i
                h, k = i // TAPS, i % TAPS
                if i == 0 and isinstance(g, int) and n < 12:
                    pe.wait_ge(w_lo_done if n else wT_done, 1)
                if k == 0 and not (isinstance(g, int) and g == 0 and j == 0):
                    pe.wait_ge(x1_done, 2 * (G * g + j - 1) + h + 1)
                if whole(g, j, i):
                    pe.wait_ge(mod_done, n + 1)
                    nc.tensor.matmul(conv_ps[h][:, :], wT[:, k * P:(k + 1) * P], pt[:, i, :], start=(k == 0),
                                     stop=(k == TAPS - 1)).then_inc(tap_done, 1)
                    return
                pe.wait_ge(lo_done, parts_before(g, j, i) + 1)
                nc.tensor.matmul(conv_ps[h][:, :], w_hi[:, k, :], pt_hi[:, i, :], start=(k == 0), stop=False)
                nc.tensor.matmul(conv_ps[h][:, :], w_hi[:, k, :], pt_lo[:, i, :], start=False, stop=False)
                nc.tensor.matmul(conv_ps[h][:, :], w_lo[:, k, :], pt_hi[:, i, :], start=False,
                                 stop=(k == TAPS - 1)).then_inc(tap_done, 1)

            def transpose_tokens(g, j, h):
                n = G * g + j
                pe.wait_ge(x1_done, 2 * n + h + 1)
                if not (isinstance(g, int) and n == 0 and h == 0):
                    pe.wait_ge(xT_out, 2 * n + h)
                for c in range(4):
                    last = nc.tensor.transpose(xT_ps[:, c * P:(c + 1) * P],
                                               x1[:, j, h * HALF + c * P:h * HALF + (c + 1) * P], ident[:, :])
                last.then_inc(xT_done, 1)

            def experts_in(g, j, h):
                n = G * g + j
                if h == 0 and past(g, j, 1):
                    pe.wait_ge(h_out, n)
                    if past(g, j, 2):
                        pe.wait_ge(hwT_out, 2 * (n - 1))
                if h == 0 and isinstance(g, int) and n == 0:
                    pe.wait_ge(aT_done, 1)
                pe.wait_ge(xT_out, 2 * n + h + 1)
                for c in range(4 * h, 4 * h + 4):
                    last = nc.tensor.matmul(h_ps, xT[:, j % 2, c, :], aT[:, c, :], start=(c == 0), stop=(c == KC - 1))
                if h == 1:
                    last.then_inc(h_done, 1)

            def transpose_hidden(g, j, newest=None, target=hwT_ps):
                pe.wait_ge(hw_done, G * g + j + 1)
                if newest is not None:
                    pe.wait_ge(h_out, newest + 1)
                nc.tensor.transpose(target, hw[:, j % 2, :], ident[:, :]).then_inc(hwT_done, 1)

            def experts_out(g, j, h, target=out_ps):
                n = G * g + j
                if h == 0 and isinstance(g, int) and n == 0:
                    pe.wait_ge(bm_lo_done, 1)
                pe.wait_ge(hwT_out, 2 * (n + 1))
                if target is out_ps and not (isinstance(g, int) and n == 0 and h == 0):
                    pe.wait_ge(out_done, 2 * n + h)
                hi, lo = hwT_hi[:, j % 2, :], hwT_lo[:, j % 2, :]
                nc.tensor.matmul(target[:, :], hi, bm_hi[:, half(h)], start=True, stop=False)
                nc.tensor.matmul(target[:, :], hi, bm_lo[:, half(h)], start=False, stop=False)
                if h == 0:
                    pe.wait_ge(hwT_rest, n + 1)
                nc.tensor.matmul(target[:, :], lo, bm_hi[:, half(h)], start=False, stop=True).then_inc(ffn_done, 1)

            def expert_means(part):
                for c in range(KC * part // 2, KC * (part + 1) // 2):
                    last = nc.tensor.matmul(out_ps[:, 0:ER + E], mean_w[:, :], aT_in[:, c, :], start=(c == 0),
                                            stop=(c == KC - 1))
                if part == 1:
                    last.then_inc(mean_done, 1)

            sum_turns = ((0, 1), (0, 4), (1, 0), (1, 3))

            pe.wait_ge(setup, 11)
            for _ in range(WARM_UP):
                nc.tensor.matmul(conv_ps[0][:, 0:P], mean_w[:, :], mean_w[:, :], start=True, stop=True)
            pe.wait_ge(onehot_in, 16)
            for j in range(G):
                sum_context(0, j)
            pe.wait_ge(ident_in, 16)
            transpose_context(0)
            pe.wait_ge(aT_in_done, 16)
            expert_means(0)
            pe.wait_ge(attn_in, 16 * 3)
            next_norms(0)
            expert_means(1)
            transpose_similarities(0)
            for i in range(2 + LEAD):
                spread_similarities(0, 0, i)

            def body(g, first, last):
                for j in range(G):
                    def before(k):
                        return (g, j - k) if j >= k else (g - 1, j - k + G)
                    one = j >= 1 or not first
                    two = j >= 2 or not first
                    three = j >= 3 or not first
                    for i in range(6):
                        if not (last and j + (i + 2 + LEAD) // 6 == G):
                            spread_similarities(*shifted(g, j, i, 2 + LEAD))
                        if i == 1 and one:
                            transpose_tokens(*before(1), 1)
                            experts_in(*before(1), 0)
                        if i == 2 and one:
                            experts_in(*before(1), 1)
                        if i == 3 and two:
                            transpose_hidden(*before(2), G * g + j - 1)
                        if i == 5 and two:
                            experts_out(*before(2), 0)
                        if i == 1 and three:
                            experts_out(*before(3), 1)
                        if i == 5:
                            transpose_tokens(g, j, 0)
                        if (j, i) in sum_turns and not last:
                            sum_context(g + 1, sum_turns.index((j, i)))
                        if i == 5 and j == 1 and not last:
                            transpose_context(g + 1)
                        if i == 4 and j == 2 and not last:
                            next_norms(g + 1)
                        if i == 0 and j == 3 and not last:
                            transpose_similarities(g + 1)
                        tap(g, j, i)

            each_group(pe, body)
            transpose_tokens(NG - 1, G - 1, 1)
            experts_in(NG - 1, G - 1, 0)
            experts_in(NG - 1, G - 1, 1)
            transpose_hidden(NG - 1, G - 2, target=last_hwT_ps[0])
            experts_out(NG - 1, G - 3, 1)
            for h in range(2):
                experts_out(NG - 1, G - 2, h, last_out_ps[h])
            transpose_hidden(NG - 1, G - 1, target=last_hwT_ps[1])
            experts_out(NG - 1, G - 1, 0, last_out_ps[2])
            experts_out(NG - 1, G - 1, 1, last_out_ps[3])



def kernel(x, ctx_4096, g_xattn, g_ffn, L0_xattn_weight, L0_ffn_router_w, L0_ffn_router_b, L0_ffn_A, L0_ffn_Bm):
    import numpy as np
    import concourse.bacc as bacc
    from concourse.bass_utils import run_bass_kernel_spmd

    x, ctx = np.ascontiguousarray(x), np.ascontiguousarray(ctx_4096)
    weight, router_w = np.asarray(L0_xattn_weight), np.asarray(L0_ffn_router_w)
    a, bm = np.asarray(L0_ffn_A), np.asarray(L0_ffn_Bm)
    B, C, T = x.shape
    E, R, _ = a.shape

    conv_wT = np.ascontiguousarray(weight.transpose(1, 2, 0)).reshape(C, TAPS * P)
    rows_a = np.concatenate([a.reshape(E * R, T), router_w], axis=0)
    expert_aT = np.ascontiguousarray(rows_a.T.reshape(T // P, P, E * R + E).transpose(1, 0, 2))
    expert_b = np.ascontiguousarray(bm.transpose(0, 2, 1)).reshape(E * R, T)

    import ml_dtypes
    bf16 = ml_dtypes.bfloat16
    identity = np.eye(P, dtype=np.float32)
    one_hot = np.zeros((P, G, 32), np.float32)
    for b in range(G):
        one_hot[:, b, b] = 1.0
    shift = np.zeros((P, 2, P), np.float32)
    shift[np.arange(1, P), 0, np.arange(P - 1)] = 1.0
    shift[0, 1, P - 1] = 1.0
    select = np.zeros((96, G, TAPS, P), np.float32)
    for c in range(C):
        for k in range(TAPS):
            block = (2, 1, 0)[(c * TAPS + k) // C]
            for part in range(3):
                for b in range(G):
                    select[32 * block + G * part + b, b, k, c] = 1.0
    expert_ids = np.tile(np.arange(E, dtype=np.float32), (P, 1))

    arrays = dict(x=x, ctx=ctx, g_xattn=np.ascontiguousarray(g_xattn), g_ffn=np.ascontiguousarray(g_ffn),
                  conv_wT=conv_wT, expert_aT=expert_aT, router_b=np.ascontiguousarray(L0_ffn_router_b),
                  expert_b=expert_b, identity=identity, identity_bf=identity.astype(bf16), one_hot=one_hot,
                  shift=shift, select=select.astype(bf16), expert_ids=expert_ids)
    nc = bacc.Bacc("TRN2", target_bir_lowering=False, num_devices=1)
    ins = {n: nc.dram_tensor(n, v.shape, mybir.dt.from_np(v.dtype), kind="ExternalInput").ap()
           for n, v in arrays.items()}
    out = nc.dram_tensor("out", x.shape, F32, kind="ExternalOutput").ap()
    flamingo_kernel(nc, **ins, out=out)
    r = run_bass_kernel_spmd(nc, [arrays], core_ids=[0])
    return r.results[0]["out"]
```
